# Optimizing a Trainium2 kernel written in Bass

```python
import numpy as np
import jax
import jax.numpy as jnp

def _softmax(x, axis=-1):
    return jax.nn.softmax(x, axis=axis)

def _gelu(x):
    return jax.nn.gelu(x, approximate=True)

def _silu(x):
    return jax.nn.silu(x)

def _sigmoid(x):
    return jax.nn.sigmoid(x)

def _layernorm(x, axis=-1, eps=1e-05):
    m = jnp.mean(x, axis=axis, keepdims=True)
    v = jnp.var(x, axis=axis, keepdims=True)
    return (x - m) / jnp.sqrt(v + eps)

def _scatter_add(tgt, idx, src, axis=0):
    return tgt.at[idx].add(src)

def _segment_sum(src, seg, n):
    return jax.ops.segment_sum(src, seg, n)
kernel_name = 'mk_flamingo_gated_d2_seqx_r8_328ff1'

def setup_inputs(seed: int=0):
    np.random.seed(seed)
    _w = jnp.asarray

    def _rec_inputs():
        import jax
        import jax.numpy as jnp
        _rk = jax.random.key(seed)
        x = -0.0002928 + 1 * jax.random.normal(jax.random.fold_in(_rk, 1), (1, 1024, 128), jnp.float32)
        _lenS = 1024 - jax.random.randint(jax.random.fold_in(_rk, 7), (1,), 0, max(1, 1024 // 4) + 1, jnp.int32)
        _lenS2 = 6404 - jax.random.randint(jax.random.fold_in(_rk, 8), (1,), 0, max(1, 6404 // 4) + 1, jnp.int32)
        _ctx_1024P = jax.random.normal(jax.random.fold_in(_rk, 11), (1, 16, 128), jnp.float32)
        _ctx_1024c = jax.random.dirichlet(jax.random.fold_in(_rk, 511), 0.3 * jnp.ones((16,), jnp.float32), (1, 6404))
        _ctx_1024t = jnp.einsum('bsk,bkd->bsd', _ctx_1024c, _ctx_1024P)
        _ctx_1024t = _ctx_1024t * jax.lax.rsqrt(jnp.mean(jnp.square(_ctx_1024t)) + 1e-12) * 0.953939
        ctx_1024 = -1.39393e-06 + 0.999914 * (_ctx_1024t + 0.3 * jax.random.normal(jax.random.fold_in(_rk, 611), (1, 6404, 128), jnp.float32))
        _validS = jnp.arange(1024)[None, :] < _lenS[:, None]
        _validS2 = jnp.arange(6404)[None, :] < _lenS2[:, None]
        _causal = jnp.tril(jnp.ones((1024, 1024), dtype=bool))
        mask_Bx1xSxS2_bf1 = jnp.ones((1, 1, 1024, 6404), dtype=bool)
        _g = jax.random.normal(jax.random.fold_in(_rk, 9001), (2, 2), jnp.float32)
        _g = jnp.sign(_g) * jnp.maximum(jnp.abs(_g), 1.0) + (_g == 0) * 1.0
        g_xattn = _g[0]
        g_ffn = _g[1]
        return (x, ctx_1024, mask_Bx1xSxS2_bf1, g_xattn, g_ffn)
    x, ctx_1024, mask_Bx1xSxS2_bf1, g_xattn, g_ffn = _rec_inputs()

    def _L0_xattn_setup():
        import jax, jax.numpy as jnp
        import numpy as np
        N_HEADS = 16
        key = jax.random.key(seed)
        ks = jax.random.split(key, 8)
        B, Tq, Tkv, C = (2, 256, 256, 128)
        std = 0.02
        return {'q': jax.random.normal(ks[0], (B, Tq, C), jnp.float32), 'k': jax.random.normal(ks[1], (B, Tkv, C), jnp.float32), 'v': jax.random.normal(ks[2], (B, Tkv, C), jnp.float32), 'Wq': jax.random.normal(ks[3], (C, C), jnp.float32) * std, 'bq': jnp.zeros((C,), jnp.float32), 'Wk': jax.random.normal(ks[4], (C, C), jnp.float32) * std, 'bk': jnp.zeros((C,), jnp.float32), 'Wv': jax.random.normal(ks[5], (C, C), jnp.float32) * std, 'bv': jnp.zeros((C,), jnp.float32), 'Wo': jax.random.normal(ks[6], (C, C), jnp.float32) * std, 'bo': jnp.zeros((C,), jnp.float32)}
    _L0_xattn_all = _L0_xattn_setup()
    _L0_xattn_in = {k: v for k, v in _L0_xattn_all.items() if k in ('Wq', 'bq', 'Wk', 'bk', 'Wv', 'bv', 'Wo', 'bo')}
    del _L0_xattn_all

    def _L0_ffn_setup():
        import jax, jax.numpy as jnp
        import numpy as np
        B, N, D, E, MULT = (4, 256, 128, 8, 4)
        F = D * MULT

        def _top2_gate(xn, Wg):
            logits = jnp.einsum('bnd,ed->bne', xn, Wg)
            probs = jax.nn.softmax(logits, axis=-1)
            top1 = jnp.argmax(probs, axis=-1)
            t1v = jnp.take_along_axis(probs, top1[..., None], axis=-1)[..., 0]
            masked = jnp.where(jax.nn.one_hot(top1, probs.shape[-1], dtype=bool), -jnp.inf, probs)
            top2 = jnp.argmax(masked, axis=-1)
            t2v = jnp.take_along_axis(masked, top2[..., None], axis=-1)[..., 0]
            denom = t1v + t2v + 1e-09
            combine = jnp.stack([t1v / denom, t2v / denom], axis=-1)
            idx = jnp.stack([top1, top2], axis=-1)
            return (combine, idx)
        key = jax.random.key(seed)
        ks = jax.random.split(key, 8)
        s_in = 1.0 / np.sqrt(D)
        s_hid = 1.0 / np.sqrt(F)
        return {'x': jax.random.normal(ks[0], (B, N, D), dtype=jnp.float32), 'gamma': jnp.ones((D,), dtype=jnp.float32), 'beta': jnp.zeros((D,), dtype=jnp.float32), 'Wg': jax.random.normal(ks[1], (E, D), dtype=jnp.float32) * s_in, 'W1': jax.random.normal(ks[2], (E, D, F), dtype=jnp.float32) * s_in, 'b1': jax.random.normal(ks[3], (E, F), dtype=jnp.float32) * 0.01, 'W2': jax.random.normal(ks[4], (E, F, D), dtype=jnp.float32) * s_hid, 'b2': jax.random.normal(ks[5], (E, D), dtype=jnp.float32) * 0.01}
    _L0_ffn_all = _L0_ffn_setup()
    _L0_ffn_in = {k: v for k, v in _L0_ffn_all.items() if k in ('gamma', 'beta', 'Wg', 'W1', 'b1', 'W2', 'b2')}
    del _L0_ffn_all

    def _L1_xattn_setup():
        import jax, jax.numpy as jnp
        import numpy as np
        EMBED = 128
        HEADS = 16
        HEAD_DIM = EMBED // HEADS
        N, S = (4, 256)
        key = jax.random.key(seed)
        ks = jax.random.split(key, 12)
        scale = 1.0 / np.sqrt(EMBED)
        inp = {'values': jax.random.normal(ks[0], (N, S, EMBED), jnp.float32), 'keys': jax.random.normal(ks[1], (N, S, EMBED), jnp.float32), 'queries': jax.random.normal(ks[2], (N, S, EMBED), jnp.float32), 'mask': jnp.ones((N, 1, S, S), dtype=bool), 'Wv': jax.random.normal(ks[3], (EMBED, EMBED), jnp.float32) * scale, 'bv': jnp.zeros((EMBED,), jnp.float32), 'Wk': jax.random.normal(ks[4], (EMBED, EMBED), jnp.float32) * scale, 'bk': jnp.zeros((EMBED,), jnp.float32), 'Wq': jax.random.normal(ks[5], (EMBED, EMBED), jnp.float32) * scale, 'bq': jnp.zeros((EMBED,), jnp.float32), 'Wo': jax.random.normal(ks[6], (EMBED, EMBED), jnp.float32) * scale, 'bo': jnp.zeros((EMBED,), jnp.float32)}
        return inp
    _L1_xattn_all = _L1_xattn_setup()
    _L1_xattn_in = {k: v for k, v in _L1_xattn_all.items() if k in ('Wv', 'bv', 'Wk', 'bk', 'Wq', 'bq', 'Wo', 'bo')}
    del _L1_xattn_all

    def _L1_ffn_setup():
        import jax, jax.numpy as jnp
        import numpy as np
        D = 128
        H = 256
        E = 8
        K = 2
        B, T = (4, 256)
        key = jax.random.key(seed)
        ks = jax.random.split(key, 7)
        s = 0.02
        return {'x': jax.random.normal(ks[0], (B, T, D), dtype=jnp.float32), 'W1': jax.random.normal(ks[1], (E, D, 2 * H), dtype=jnp.float32) * s, 'b1': jnp.zeros((E, 2 * H), dtype=jnp.float32), 'W2': jax.random.normal(ks[2], (E, H, D), dtype=jnp.float32) * s, 'b2': jnp.zeros((E, D), dtype=jnp.float32), 'Wr': jax.random.normal(ks[3], (D, E), dtype=jnp.float32) * s, 'br': jnp.zeros((E,), dtype=jnp.float32)}
    _L1_ffn_all = _L1_ffn_setup()
    _L1_ffn_in = {k: v for k, v in _L1_ffn_all.items() if k in ('W1', 'b1', 'W2', 'b2', 'Wr', 'br')}
    del _L1_ffn_all
    return {'x': x, 'ctx_1024': ctx_1024, 'mask_Bx1xSxS2_bf1': mask_Bx1xSxS2_bf1, 'g_xattn': g_xattn, 'g_ffn': g_ffn, 'L0_xattn_Wq': _L0_xattn_in['Wq'], 'L0_xattn_bq': _L0_xattn_in['bq'], 'L0_xattn_Wk': _L0_xattn_in['Wk'], 'L0_xattn_bk': _L0_xattn_in['bk'], 'L0_xattn_Wv': _L0_xattn_in['Wv'], 'L0_xattn_bv': _L0_xattn_in['bv'], 'L0_xattn_Wo': _L0_xattn_in['Wo'], 'L0_xattn_bo': _L0_xattn_in['bo'], 'L0_ffn_gamma': _L0_ffn_in['gamma'], 'L0_ffn_beta': _L0_ffn_in['beta'], 'L0_ffn_Wg': _L0_ffn_in['Wg'], 'L0_ffn_W1': _L0_ffn_in['W1'], 'L0_ffn_b1': _L0_ffn_in['b1'], 'L0_ffn_W2': _L0_ffn_in['W2'], 'L0_ffn_b2': _L0_ffn_in['b2'], 'L1_xattn_Wv': _L1_xattn_in['Wv'], 'L1_xattn_bv': _L1_xattn_in['bv'], 'L1_xattn_Wk': _L1_xattn_in['Wk'], 'L1_xattn_bk': _L1_xattn_in['bk'], 'L1_xattn_Wq': _L1_xattn_in['Wq'], 'L1_xattn_bq': _L1_xattn_in['bq'], 'L1_xattn_Wo': _L1_xattn_in['Wo'], 'L1_xattn_bo': _L1_xattn_in['bo'], 'L1_ffn_W1': _L1_ffn_in['W1'], 'L1_ffn_b1': _L1_ffn_in['b1'], 'L1_ffn_W2': _L1_ffn_in['W2'], 'L1_ffn_b2': _L1_ffn_in['b2'], 'L1_ffn_Wr': _L1_ffn_in['Wr'], 'L1_ffn_br': _L1_ffn_in['br']}

def reference(x, ctx_1024, mask_Bx1xSxS2_bf1, g_xattn, g_ffn, L0_xattn_Wq, L0_xattn_bq, L0_xattn_Wk, L0_xattn_bk, L0_xattn_Wv, L0_xattn_bv, L0_xattn_Wo, L0_xattn_bo, L0_ffn_gamma, L0_ffn_beta, L0_ffn_Wg, L0_ffn_W1, L0_ffn_b1, L0_ffn_W2, L0_ffn_b2, L1_xattn_Wv, L1_xattn_bv, L1_xattn_Wk, L1_xattn_bk, L1_xattn_Wq, L1_xattn_bq, L1_xattn_Wo, L1_xattn_bo, L1_ffn_W1, L1_ffn_b1, L1_ffn_W2, L1_ffn_b2, L1_ffn_Wr, L1_ffn_br):
    import jax
    import jax.numpy as jnp

    def _L0_xattn_ref(q, k, v, Wq, bq, Wk, bk, Wv, bv, Wo, bo):
        import jax, jax.numpy as jnp
        import numpy as np
        N_HEADS = 16
        b, t, c = q.shape
        h = N_HEADS
        d = c // h
        scale = d ** (-0.5)
        qh = (q @ Wq.T + bq).reshape(b, t, h, d).transpose(0, 2, 1, 3)
        kh = (k @ Wk.T + bk).reshape(b, -1, h, d).transpose(0, 2, 1, 3)
        vh = (v @ Wv.T + bv).reshape(b, -1, h, d).transpose(0, 2, 1, 3)
        attn = jnp.einsum('bhtd,bhsd->bhts', qh, kh) * scale
        attn = jax.nn.softmax(attn, axis=-1)
        out = jnp.einsum('bhts,bhsd->bhtd', attn, vh)
        out = out.transpose(0, 2, 1, 3).reshape(b, t, c)
        return out @ Wo.T + bo

    def _L0_ffn_ref(x, gamma, beta, Wg, W1, b1, W2, b2):
        import jax, jax.numpy as jnp
        import numpy as np
        B, N, D, E, MULT = (4, 256, 128, 8, 4)
        F = D * MULT

        def _top2_gate(xn, Wg):
            logits = jnp.einsum('bnd,ed->bne', xn, Wg)
            probs = jax.nn.softmax(logits, axis=-1)
            top1 = jnp.argmax(probs, axis=-1)
            t1v = jnp.take_along_axis(probs, top1[..., None], axis=-1)[..., 0]
            masked = jnp.where(jax.nn.one_hot(top1, probs.shape[-1], dtype=bool), -jnp.inf, probs)
            top2 = jnp.argmax(masked, axis=-1)
            t2v = jnp.take_along_axis(masked, top2[..., None], axis=-1)[..., 0]
            denom = t1v + t2v + 1e-09
            combine = jnp.stack([t1v / denom, t2v / denom], axis=-1)
            idx = jnp.stack([top1, top2], axis=-1)
            return (combine, idx)
        residual = x
        mu = jnp.mean(x, axis=-1, keepdims=True)
        var = jnp.mean(jnp.square(x - mu), axis=-1, keepdims=True)
        xn = (x - mu) / jnp.sqrt(var + 1e-05) * gamma + beta
        combine, idx = _top2_gate(xn, Wg)
        n_expert = Wg.shape[0]
        onehot = jax.nn.one_hot(idx, n_expert, dtype=x.dtype)
        gates = jnp.einsum('bns,bnse->ebn', combine, onehot)

        def body(acc, params):
            w1, b1e, w2, b2e, g = params
            h = jax.nn.gelu(jnp.einsum('bnd,df->bnf', xn, w1) + b1e, approximate=True)
            y = jnp.einsum('bnf,fd->bnd', h, w2) + b2e
            return (acc + g[..., None] * y, None)
        out, _ = jax.lax.scan(body, jnp.zeros_like(x), (W1, b1, W2, b2, gates))
        return residual + out

    def _L1_xattn_ref(values, keys, queries, mask, Wv, bv, Wk, bk, Wq, bq, Wo, bo):
        import jax, jax.numpy as jnp
        import numpy as np
        EMBED = 128
        HEADS = 16
        HEAD_DIM = EMBED // HEADS
        N, S = (4, 256)
        n, q_len = (queries.shape[0], queries.shape[1])
        v = (values @ Wv.T + bv).reshape(n, -1, HEADS, HEAD_DIM)
        k = (keys @ Wk.T + bk).reshape(n, -1, HEADS, HEAD_DIM)
        q = (queries @ Wq.T + bq).reshape(n, -1, HEADS, HEAD_DIM)
        energy = jnp.einsum('nqhd,nkhd->nhqk', q, k)
        energy = jnp.where(mask, energy, jnp.float32(-1e+20))
        attn = jax.nn.softmax(energy / np.sqrt(HEAD_DIM), axis=-1)
        out = jnp.einsum('nhqk,nkhd->nqhd', attn, v).reshape(n, q_len, EMBED)
        return out @ Wo.T + bo

    def _L1_ffn_ref(x, W1, b1, W2, b2, Wr, br):
        import jax, jax.numpy as jnp
        import numpy as np
        D = 128
        H = 256
        E = 8
        K = 2
        B, T = (4, 256)
        Bb, Tt, Dd = x.shape
        xf = x.reshape(-1, Dd)
        logits = xf @ Wr + br
        topk_val, topk_idx = jax.lax.top_k(logits, K)
        scores = jax.nn.softmax(topk_val, axis=-1)
        h = jnp.einsum('nd,edh->enh', xf, W1) + b1[:, None, :]
        a, g = jnp.split(h, 2, axis=-1)
        act = jax.nn.silu(a) * g
        out_e = jnp.einsum('enh,ehd->end', act, W2) + b2[:, None, :]
        out_ne = out_e.transpose(1, 0, 2)
        gathered = jnp.take_along_axis(out_ne, topk_idx[:, :, None], axis=1)
        out = jnp.sum(gathered * scores[:, :, None], axis=1)
        return out.reshape(Bb, Tt, Dd)
    x = x + jnp.tanh(g_xattn[0]) * _L0_xattn_ref(_layernorm(x, axis=-1), ctx_1024, ctx_1024, L0_xattn_Wq, L0_xattn_bq, L0_xattn_Wk, L0_xattn_bk, L0_xattn_Wv, L0_xattn_bv, L0_xattn_Wo, L0_xattn_bo)
    x = x + jnp.tanh(g_ffn[0]) * _L0_ffn_ref(_layernorm(x, axis=-1), L0_ffn_gamma, L0_ffn_beta, L0_ffn_Wg, L0_ffn_W1, L0_ffn_b1, L0_ffn_W2, L0_ffn_b2)
    x = x + jnp.tanh(g_xattn[1]) * _L1_xattn_ref(ctx_1024, ctx_1024, _layernorm(x, axis=-1), mask_Bx1xSxS2_bf1, L1_xattn_Wv, L1_xattn_bv, L1_xattn_Wk, L1_xattn_bk, L1_xattn_Wq, L1_xattn_bq, L1_xattn_Wo, L1_xattn_bo)
    x = x + jnp.tanh(g_ffn[1]) * _L1_ffn_ref(_layernorm(x, axis=-1), L1_ffn_W1, L1_ffn_b1, L1_ffn_W2, L1_ffn_b2, L1_ffn_Wr, L1_ffn_br)
    return x

_drawn_inputs = setup_inputs


def setup_inputs(seed=0):
    import zlib

    import numpy as np

    out = dict(_drawn_inputs(seed))
    spreads = {'g_ffn': (-1.0, 0.6),
     'L0_xattn_bq': (0.0, 0.8),
     'L0_xattn_bk': (0.0, 2.0),
     'L0_xattn_bv': (0.0, 0.1),
     'L0_xattn_bo': (0.0, 0.1),
     'L0_ffn_gamma': (1.0, 0.2),
     'L0_ffn_beta': (0.0, 0.1),
     'L1_xattn_bv': (0.0, 0.1),
     'L1_xattn_bk': (0.0, 2.0),
     'L1_xattn_bq': (0.0, 0.1),
     'L1_xattn_bo': (0.0, 0.1),
     'L1_ffn_b1': (0.0, 0.8),
     'L1_ffn_b2': (0.0, 0.331),
     'L1_ffn_br': (0.0, 0.1)}
    factors = {'L0_xattn_Wq': 8.0,
     'L0_xattn_Wk': 8.0,
     'L0_ffn_b1': 6.533,
     'L0_ffn_b2': 4.78,
     'L1_ffn_W1': 6.642,
     'L1_ffn_W2': 6.313}
    for name, (base, spread) in spreads.items():
        noise = np.random.default_rng([zlib.crc32(name.encode()), seed]).standard_normal(out[name].shape)
        drawn = base * np.exp(spread * noise) if base else spread * noise
        out[name] = jnp.asarray(drawn.astype(out[name].dtype))
    for name, factor in factors.items():
        out[name] = (out[name] * factor).astype(out[name].dtype)
    return out
```

```python
from contextlib import ExitStack

import concourse.bass as bass
import numpy as np
from concourse import mybir

F32 = mybir.dt.float32
BF16 = mybir.dt.bfloat16
F8 = mybir.dt.float8e5
U8 = mybir.dt.uint8
U16 = mybir.dt.uint16
I32 = mybir.dt.int32
ALU = mybir.AluOpType
ACT = mybir.ActivationFunctionType
AX = mybir.AxisListType

P = 128
C = 128
H = 16
HD = C // H
TQ = 1024
TK = 6404
QT = TQ // P
NFULL = TK // P
TAIL = TK - NFULL * P
NT = NFULL + 1
HALF = 512
E = 8
FF = 512
EPS = 1e-5
SCALE = float(HD) ** -0.5
MASKED = -1e20

PARTS = 3
KR = PARTS * HD
QKR = PARTS * KR
MROW = 96
ROWS_MAX = MROW
ROWS_EXP = MROW + PARTS
VW = HD + 1
QG = 4
QGW = TQ // QG
RING = 3
STEP = 2
NSTEP = NT // STEP
STEP_TILES = [range(STEP * s, STEP * s + STEP if s < NSTEP - 1 else NT) for s in range(NSTEP)]
PSLOTS = 5
EXB = 3
V_CHUNKS = [(0, 12), (12, 24), (24, 36), (36, NT)]
AHEAD = 6
ENDING = [("next", 0), "turn", ("next", 1), ("next", 2), ("next", 3), "rows", ("next", 4), ("next", 5)]
AFTER_ROWS = 2
MXU = NT + 3


def mx_steps(ahead):
    tiles = [("max", t) for t in range(AHEAD, NT)]
    units = tiles + [u for u in ENDING if ahead or isinstance(u, str)]
    steps = [units[2 * s:2 * s + 2] for s in range(NSTEP - 2)]
    rest = units[2 * (NSTEP - 2):]
    cut = len(rest) // 2
    steps += [rest[:cut], rest[cut:]]
    steps[1] = steps[1] + ["out"]
    return steps


assert NT == NSTEP * STEP + 1 and MXU % 2 == 0 and AHEAD % 2 == 0 and 2 * NT % EXB == 0 and NT % PSLOTS == 1
MCH = 10


def width(t):
    return P if t < NFULL else TAIL


def block_kernel(nc, a, out):
    with ExitStack() as ctx:
        def sb(name, shape, dt=F32):
            return ctx.enter_context(nc.sbuf_tensor(name, shape, dt))

        sems = {}

        def sem(name):
            if name not in sems:
                sems[name] = ctx.enter_context(nc.semaphore(name))
            return sems[name]

        k_parts = [nc.dram_tensor(f"k_parts{l}", [C, PARTS, TK], BF16, kind="Internal").ap() for l in range(2)]
        q_rows = [nc.dram_tensor(f"q_rows{l}", [H, PARTS, HD, PARTS, TQ], BF16, kind="Internal").ap() for l in range(2)]
        gate_rows = [nc.dram_tensor(f"gate_rows{l}", [E, TQ], F32, kind="Internal").ap() for l in range(2)]

        ps = ctx.enter_context(nc.psum_tensor("ps", [P, 8, HALF], F32))

        def flat3(t):
            return t[:, :, :].rearrange("p a b -> p (a b)")

        ctx_t = sb("ctx_t", [P, TK])
        w1_1 = ctx_t[:, 0:E * FF].rearrange("p (e f) -> p e f", e=E)
        w2_1 = ctx_t[:, E * FF:E * FF + E * 2 * C].rearrange("p (e t d) -> p e t d", e=E, t=2)
        k_ring = sb("k_ring", [P, RING * TK], BF16)
        q_ring = sb("q_ring", [P, RING * TQ], BF16)
        gate_bc = k_ring[:, 0:E * TQ * 2].bitcast(F32).rearrange("p (e q) -> p e q", e=E)
        v_all = sb("v_all", [P, NT, H, VW])
        v_head = sb("v_head", [P, NT, VW])
        probs = sb("probs", [P, PSLOTS + 1, TQ])
        m_join = probs[:, PSLOTS, :]
        mask_stage = probs[:, 0:3, :].rearrange("p a b -> p (a b)")[:, 0:MCH * TQ // 4].bitcast(U8)
        mask_junk = probs[:, 3:6, :].rearrange("p a b -> p (a b)")[:, 0:MCH * TQ // 4].bitcast(BF16)
        h_ring = probs[:, 0:2, :].rearrange("p a (b c) -> p (a b) c", b=2)
        hg_ring = probs[:, 2:6, :].rearrange("p a (b c) -> p (a b) c", b=2)
        big = sb("big", [P, NT * TQ // 4])
        w1_0 = big[:, 0:E * FF].rearrange("p (e f) -> p e f", e=E)
        w2_0 = big[:, E * FF:2 * E * FF].rearrange("p (e t d) -> p e t d", e=E, t=4)
        mask_n = big[:, :].bitcast(F8).rearrange("p (t q) -> p t q", t=NT)
        spare = big[:, 2 * E * FF:]
        k_f = spare[:, 0:2 * HALF].rearrange("p (a w) -> p a w", a=2)
        k_rest = spare[:, 2 * HALF:4 * HALF].rearrange("p (a w) -> p a w", a=2)
        k_st = spare[:, 4 * HALF:7 * HALF].bitcast(BF16).rearrange("p (a b w) -> p a b w", a=2, b=PARTS)
        gate_t = spare[0:E, 7 * HALF:7 * HALF + TQ]
        q_f = k_f
        m_run = sb("m_run", [P, 2, TQ])
        x_t = m_run[:, 0, :]
        y_t = m_run[:, 1, :]
        x_n = y_t.rearrange("p (t c) -> p t c", c=C)
        x_sb = sb("x_sb", [P, QT, C])
        o_all = sb("o_all", [P, QT, (H + 1) * HD])
        x_ln = flat3(o_all)[:, 0:QT * C].rearrange("p (t c) -> p t c", c=C)
        o_raw = sb("o_raw", [P, QGW])
        m_neg = sb("m_neg", [P, 2, QT])
        m_pad = sb("m_pad", [P, QT, P], BF16)
        r_den = sb("r_den", [P, QT])
        w_att = sb("w_att", [P, 2, 4, C])
        b_col = sb("b_col", [P, 2, 2])
        b_row = sb("b_row", [P, 2, 2, C])
        gb_row = sb("gb_row", [P, 2, C])
        w_gate = sb("w_gate", [P, 2, E])
        br_row = sb("br_row", [P, E])
        b1_col = sb("b1_col", [P, 2, E * 4])
        b2_sb = sb("b2_sb", [E, 2, C])
        g_raw = sb("g_raw", [P, 4])
        g_tanh = sb("g_tanh", [P, 4])
        ident_f = sb("ident_f", [P, P])
        ident_b = sb("ident_b", [P, P], BF16)
        neg_i = sb("neg_i", [P, P], BF16)
        ones_f = sb("ones_f", [P, 1])
        zeros_b = sb("zeros_b", [P, QGW], BF16)
        rank = sb("rank", [P, E])
        st = sb("st", [P, QT, 6])
        mv = sb("mv", [P, QT, 2])
        var_e = sb("var_e", [P, QT])
        std = sb("std", [P, QT])
        r_std = sb("r_std", [P, QT])
        ga = sb("ga", [P, 6, QT, E])
        gs = sb("gs", [P, 6, QT])
        m_sum = sb("m_sum", [P, 8])
        m_tot = sb("m_tot", [P, 1])
        flag_f = sb("flag_f", [1, 1])
        flag = sb("flag", [1, 1], I32)

        def mx(slot):
            return ps[:, 2 * slot:2 * slot + 2, :]

        def flat(ap):
            return ap.rearrange("p a b -> p (a b)")

        NCH = -(-TK // HALF)
        chunk_w = [min(HALF, TK - HALF * c) for c in range(NCH)]
        ATT_IN, SMALL_IN = 16 * 16, 16 * 9
        FIRST = NT + len(ENDING)
        LOOP = H - 2
        LAST2 = FIRST + MXU * LOOP
        LAST = LAST2 + MXU - AHEAD
        MX_OUT = sum(len(u) for u in mx_steps(True)[:2])


        def wait_apart(eng, name, s, value, apart=True):
            eng.wait_ge(s, value)
            if apart and not isinstance(value, int):
                eng.sem_inc(sem(f"{name}_apart"), 1)

        block = ctx.enter_context(nc.Block())

        @block.sync
        def _(sp):
            def setup():
                for l in range(2):
                    for n, w in enumerate("qkvo"):
                        sp.dma_start(w_att[:, l, n, :], a[f"w{w}{l}"]).then_inc(sem("att_w_in"), 16)
                    for n, w in enumerate("qk"):
                        sp.dma_start(b_col[:, l, n:n + 1], a[f"b{w}{l}"]).then_inc(sem("att_w_in"), 16)
                    for n, w in enumerate("vo"):
                        sp.dma_start(b_row[:, l, n, :], a[f"b{w}{l}"].partition_broadcast(P)).then_inc(sem("att_w_in"), 16)
                for c0, c1 in ((0, 2048), (2048, TK)):
                    sp.dma_start(ctx_t[:, c0:c1], a["ctx_t"][:, c0:c1]).then_inc(sem(f"ctx_in{c0}"), 16)
                sp.dma_start(g_raw[:, 0:2], a["g_xattn"].partition_broadcast(P)).then_inc(sem("g_in"), 16)
                sp.dma_start(g_raw[:, 2:4], a["g_ffn"].partition_broadcast(P)).then_inc(sem("g_in"), 16)
                for l in range(2):
                    sp.dma_start(w_gate[:, l, :], a[f"w_gate{l}"]).then_inc(sem("small_in"), 16)
                    sp.dma_start(b1_col[:, l, :], a[f"b1_{l}"]).then_inc(sem("small_in"), 16)
                    sp.dma_start(b2_sb[:, l, :], a[f"b2_{l}"]).then_inc(sem("small_in"), 16)
                for n, w in enumerate(("gamma", "beta")):
                    sp.dma_start(gb_row[:, n, :], a[w].partition_broadcast(P)).then_inc(sem("small_in"), 16)
                sp.dma_start(br_row[:, :], a["br"].partition_broadcast(P)).then_inc(sem("small_in"), 16)
                sp.dma_start(w1_0, a["w1_0"].rearrange("e d f -> d e f")).then_inc(sem("experts_in0"), 16)
                sp.dma_start(w2_0.rearrange("p e t d -> p (e t) d"),
                             a["w2_0"].rearrange("e (t f) d -> f (e t) d", f=P)).then_inc(sem("experts_in0"), 16)

            def store_k(l):
                for c in range(NCH):
                    sp.wait_ge(sem(f"k_split{l}"), c + 1)
                    sp.dma_start(k_parts[l][:, :, HALF * c:HALF * c + chunk_w[c]],
                                 k_st[:, c % 2, :, 0:chunk_w[c]]).then_inc(sem(f"k_stored{l}_{c % 2}"), 16)

            def store_q(l):
                for half in range(2):
                    sp.wait_ge(sem(f"q_split{l}"), half + 1)
                    for b in range(PARTS):
                        for d in range(PARTS):
                            sp.dma_start(q_rows[l].rearrange("h b d a w -> b a h d w")[b, d][:, :, HALF * half:HALF * half + HALF],
                                         k_st[:, half, b, :]).then_inc(sem(f"q_stored{l}"), 16)

            def check_mask():
                for c in range(NFULL // MCH):
                    if c:
                        sp.wait_ge(sem("mask_summed"), c)
                    sp.dma_start(mask_stage.rearrange("p (t q) -> p t q", q=TQ),
                                 a["mask_t"][c * MCH * P:(c + 1) * MCH * P, :].rearrange("(t p) q -> p t q", p=P)
                                 ).then_inc(sem("mask_in"), 16)
                sp.wait_ge(sem("mask_summed"), NFULL // MCH)
                sp.dma_start(mask_stage[0:TAIL, 0:TQ], a["mask_t"][NFULL * P:TK, :]).then_inc(sem("mask_in"), 16)

            def build_mask():
                sp.wait_ge(sem("flag_ready"), 1)
                sp.wait_ge(sem("ffn_done0"), 1)
                with sp.If(sp.value_load(flag[0:1, 0:1], min_val=0, max_val=1) > 0):
                    for c in range(NFULL // MCH):
                        if c:
                            sp.wait_ge(sem("mask_turned"), c)
                        sp.dma_start(mask_stage.rearrange("p (t q) -> p t q", q=TQ),
                                     a["mask_t"][c * MCH * P:(c + 1) * MCH * P, :].rearrange("(t p) q -> p t q", p=P)
                                     ).then_inc(sem("mask_again"), 16)
                    sp.wait_ge(sem("mask_turned"), NFULL // MCH)
                    sp.dma_start(mask_stage[0:TAIL, 0:TQ], a["mask_t"][NFULL * P:TK, :]).then_inc(sem("mask_again"), 16)
                with sp.Else():
                    sp.nop()

            def load_head(l, h):
                def place(w):
                    return h % RING * w if isinstance(h, int) else sp.snap((h % RING) * w)

                koff, qoff = place(TK), place(TQ)
                if not isinstance(h, int):
                    wait_apart(sp, "sp", sem(f"scored{l}"), h * (2 * NT) - (RING - 1) * 2 * NT)
                for b in range(PARTS):
                    sp.dma_start(k_ring[b * KR:(b + 1) * KR, bass.ds(koff, TK)],
                                 k_parts[l][bass.ds(h * HD, HD)].rearrange("d a w -> (d a) w")
                                 ).then_inc(sem(f"head_in{l}"), 16)
                sp.dma_start(q_ring[0:QKR, bass.ds(qoff, TQ)],
                             q_rows[l][bass.ds(h, 1)].rearrange("h b d a w -> (h b d a) w")).then_inc(sem(f"head_in{l}"), 16)

            def load_heads(l):
                sp.wait_ge(sem("ring_set"), 2 * (l + 1))
                sp.wait_ge(sem(f"k_stored{l}_0"), 16 * (-(-NCH // 2)))
                sp.wait_ge(sem(f"k_stored{l}_1"), 16 * (NCH // 2))
                sp.wait_ge(sem(f"q_stored{l}"), 16 * 18)
                for h in range(RING):
                    load_head(l, h)
                    sp.wait_ge(sem(f"head_in{l}"), 64 * (h + 1))
                with sp.Fori(RING, H) as h:
                    load_head(l, h)
                    wait_apart(sp, "sp", sem(f"head_in{l}"), 64 * h + 64)

            def spread_gates(l):
                sp.wait_ge(sem(f"gate_t{l}"), 1)
                sp.dma_start(gate_rows[l], gate_t[:, :]).then_inc(sem(f"gate_out{l}"), 16)
                sp.wait_ge(sem(f"gate_out{l}"), 16)
                for e in range(E):
                    sp.dma_start(gate_bc[:, e, :], gate_rows[l][e:e + 1, :].rearrange("e q -> (e q)").partition_broadcast(P)
                                 ).then_inc(sem(f"gate_bc{l}_{e}"), 16)

            setup()
            sp.dma_start(x_sb[:, :, :], a["x"].rearrange("(t p) c -> p t c", p=P)).then_inc(sem("x_in"), 16)
            store_k(0)
            store_q(0)
            check_mask()
            load_heads(0)
            store_k(1)
            sp.wait_ge(sem("v_proj1"), NCH)
            sp.wait_ge(sem("k_proj1"), NCH)
            sp.dma_start(w1_1, a["w1_1"].rearrange("e d f -> d e f")).then_inc(sem("experts_in1"), 16)
            sp.dma_start(w2_1.rearrange("p e t d -> p (e t) d"),
                         a["w2_1"].rearrange("e (t f) d -> f (e t) d", f=P)).then_inc(sem("experts_in1"), 16)
            spread_gates(0)
            store_q(1)
            build_mask()
            load_heads(1)
            spread_gates(1)
            sp.wait_ge(sem("x_final"), 1)
            sp.dma_start(out.rearrange("(t p) c -> p t c", p=P), x_sb[:, :, :]).then_inc(sem("out_stored"), 16)
            sp.wait_ge(sem("out_stored"), 16)

        @block.gpsimd
        def _(pool):
            chain = [0]

            def link(ins):
                chain[0] += 1
                ins.then_inc(sem("pool_chain"), 1)
                pool.wait_ge(sem("pool_chain"), chain[0])

            def constants():
                link(nc.gpsimd.memset(ident_f[:, :], 0.0))
                nc.gpsimd.affine_select(out=ident_f[:, :], in_=ident_f[:, :], compare_op=ALU.not_equal, fill=1.0,
                                        base=0, pattern=[[-1, P]], channel_multiplier=1).then_inc(sem("ident"), 1)
                pool.wait_ge(sem("ident"), 1)
                nc.gpsimd.tensor_copy(ident_b[:, :], ident_f[:, :]).then_inc(sem("ident"), 1)
                link(nc.gpsimd.memset(v_all[:, :, :, :], 1.0))
                nc.gpsimd.memset(zeros_b[:, :], 0.0).then_inc(sem("v_ones"), 1)
                for e in range(E):
                    nc.gpsimd.memset(rank[:, e:e + 1], float(E - e)).then_inc(sem("rank"), 1)
                nc.gpsimd.memset(ones_f[:, :], 1.0).then_inc(sem("rank"), 1)
                nc.gpsimd.memset(m_pad[:, :, :], 0.0).then_inc(sem("rank"), 1)
                nc.gpsimd.tensor_scalar(neg_i[:, :], ident_f[:, :], MASKED, 0.0, ALU.mult, ALU.add).then_inc(sem("rank"), 1)
                pool.wait_ge(sem("rank"), E + 3)

            def set_ring(l):
                nc.gpsimd.memset(q_ring[2 * 32:MROW, :], 0.0).then_inc(sem("ring_z"), 1)
                pool.wait_ge(sem("ring_z"), l + 1)
                nc.gpsimd.memset(k_ring[2 * 32:MROW, :], 0.0).then_inc(sem("ring_set"), 1)
                pool.wait_ge(sem("ring_set"), 2 * l + 1)
                nc.gpsimd.memset(k_ring[MROW:P, :], 1.0).then_inc(sem("ring_set"), 1)
                pool.wait_ge(sem("ring_set"), 2 * l + 2)

            def v_chunk(l, h, n):
                t0, t1 = V_CHUNKS[n]
                nc.gpsimd.tensor_copy(v_head[:, t0:t1, :], v_all[:, t0:t1, bass.ds(h, 1), :].rearrange("p t o d -> p t (o d)")
                                      ).then_inc(sem(f"v_head{l}"), 1)

            def v_heads(l):
                pool.wait_ge(sem(f"v_set{l}"), NCH + 1)
                for n in range(len(V_CHUNKS)):
                    v_chunk(l, 0, n)
                with pool.Fori(1, H) as h:
                    for n, (_, t1) in enumerate(V_CHUNKS):
                        pool.wait_ge(sem(f"pv_done{l}"), h * NT + (1 - NT + t1))
                        v_chunk(l, h, n)

            constants()
            set_ring(0)
            v_heads(0)
            pool.wait_ge(sem("v_head0"), H * len(V_CHUNKS))
            pool.wait_ge(sem("ffn_done0"), 1)
            set_ring(1)
            v_heads(1)

        @block.scalar
        def _(act):
            A = nc.scalar.activation

            def project_k(l):
                if l:
                    act.wait_ge(sem("q_split0"), 2)
                    act.wait_ge(sem("q_stored0"), 16 * 18)
                for c in range(NCH):
                    w = chunk_w[c]
                    act.wait_ge(sem(f"k_proj{l}"), c + 1)
                    if c >= 2:
                        act.wait_ge(sem(f"k_split{l}"), c - 1)
                        act.wait_ge(sem(f"k_stored{l}_{c % 2}"), 16 * (c // 2))
                    A(k_f[:, c % 2, 0:w], ps[:, c % 2, 0:w], ACT.Identity, bias=b_col[:, l, 1:2]).then_inc(sem(f"k_evac{l}"), 1)
                    A(k_st[:, c % 2, 0, 0:w], ps[:, c % 2, 0:w], ACT.Identity, bias=b_col[:, l, 1:2]).then_inc(sem(f"k_evac{l}"), 1)

            def std_of(tag):
                act.wait_ge(sem(f"var_{tag}"), 1)
                A(std[:, :], var_e[:, :], ACT.Sqrt).then_inc(sem(f"std_{tag}"), 1)

            def turned(tag, bank, dst):
                act.wait_ge(sem(f"turned_{tag}"), 2)
                A(dst, flat(ps[:, bank:bank + 2, :]), ACT.Identity).then_inc(sem(f"copied_{tag}"), 1)

            def project_q(l):
                turned(f"q{l}", 4, x_t)
                act.wait_ge(sem(f"k_split{l}"), NCH)
                act.wait_ge(sem(f"k_stored{l}_0"), 16 * (-(-NCH // 2)))
                act.wait_ge(sem(f"k_stored{l}_1"), 16 * (NCH // 2))
                for half in range(2):
                    act.wait_ge(sem(f"q_proj{l}"), half + 1)
                    A(q_f[:, half, :], ps[:, 6 + half, :], ACT.Identity, bias=b_col[:, l, 0:1]).then_inc(sem(f"q_evac{l}"), 1)
                    A(k_st[:, half, 0, :], ps[:, 6 + half, :], ACT.Identity, bias=b_col[:, l, 0:1]).then_inc(sem(f"q_evac{l}"), 1)

            def sum_mask():
                for c in range(NFULL // MCH + 1):
                    act.wait_ge(sem("mask_in"), 16 * (c + 1))
                    rows, n = (P, MCH * TQ // 2) if c < NFULL // MCH else (TAIL, TQ // 2)
                    if c:
                        act.wait_ge(sem("mask_summed"), c)
                    A(mask_junk[0:rows, 0:n], mask_stage[0:rows, 0:2 * n].bitcast(U16), ACT.Copy,
                      accum_out=m_sum[0:rows, c:c + 1]).then_inc(sem("mask_summed"), 1)
                act.wait_ge(sem("mask_summed"), NFULL // MCH + 1)

            def exp_head(l, h, out_unit):
                for t in range(NT):
                    k = width(t)
                    if t >= PSLOTS:
                        act.wait_ge(sem(f"pv_done{l}"), h * NT + (t - PSLOTS + 2))
                    for half in range(2):
                        u = 2 * t + half
                        act.wait_ge(sem(f"scored{l}"), h * (2 * NT) + (u + 1))
                        A(probs[0:k, t % PSLOTS, HALF * half:HALF * half + HALF], ps[0:k, 4 + u % EXB, :], ACT.Exp,
                          scale=SCALE).then_inc(sem(f"exp_done{l}"), 1)
                act.wait_ge(sem(f"pv_done{l}"), h * NT + (NT + 1))
                act.wait_ge(sem(f"mx_filled{l}"), out_unit)
                A(o_raw[:, :], ps[:, 7, 0:QGW], ACT.Identity).then_inc(sem(f"o_raw{l}"), 1)

            def exp_all(l):
                act.nop().then_inc(sem(f"exp_done{l}"), EXB)
                with act.Fori(0, LOOP) as h:
                    exp_head(l, h, h * MXU + (FIRST + MX_OUT))
                exp_head(l, H - 2, LAST2 + MX_OUT)
                exp_head(l, H - 1, LAST + 1)

            def gates(l):
                act.wait_ge(sem(f"gate_in{l}"), 1)
                A(ga[:, 1, :, :], ga[:, 0, :, :], ACT.Exp).then_inc(sem(f"gate_exp{l}"), 1)

            def gates_turned(l):
                act.wait_ge(sem(f"gate_turned{l}"), 1)
                A(gate_t[:, :], flat(ps[0:E, 2:4, :]), ACT.Identity).then_inc(sem(f"gate_t{l}"), 1)

            def experts0():
                for u in range(E * 2 * 4):
                    e, t = u // 8, u % 4
                    act.wait_ge(sem("hidden0"), u + 1)
                    if u >= 4:
                        act.wait_ge(sem("gated0"), u - 3)
                    A(h_ring[:, u % 4, :], ps[:, u % 4, :], ACT.Gelu_apprx_tanh,
                      bias=b1_col[:, 0, e * 4 + t:e * 4 + t + 1]).then_inc(sem("act_done0"), 1)

            def experts1():
                for u in range(E * 2):
                    e = u // 2
                    act.wait_ge(sem("hidden1"), 4 * u + 2)
                    for t in range(2):
                        if u >= 2:
                            act.wait_ge(sem("gated1"), 2 * (u - 2) + t + 1)
                        A(h_ring[:, 2 * (u % 2) + t, :], ps[:, t, :], ACT.Silu,
                          bias=b1_col[:, 1, e * 4 + t:e * 4 + t + 1]).then_inc(sem("act_done1"), 1)

            def y_out(l):
                act.wait_ge(sem(f"down{l}"), 2 * E * (4, 2)[l])
                A(y_t, flat(ps[:, 4:6, :]), ACT.Identity).then_inc(sem(f"y_t{l}"), 1)

            act.wait_ge(sem("g_in"), 32)
            A(g_tanh[:, :], g_raw[:, :], ACT.Tanh).then_inc(sem("g_tanh"), 1)
            act.wait_ge(sem("att_w_in"), ATT_IN)
            std_of("q0")
            project_k(0)
            project_q(0)
            sum_mask()
            exp_all(0)
            turned("o0", 0, x_t)
            project_k(1)
            std_of("f0")
            std_of("g0")
            turned("f0", 0, x_t)
            gates(0)
            gates_turned(0)
            experts0()
            y_out(0)
            std_of("q1")
            project_q(1)
            exp_all(1)
            turned("o1", 0, x_t)
            std_of("f1")
            turned("f1", 0, x_t)
            gates(1)
            gates_turned(1)
            experts1()
            y_out(1)

        @block.vector
        def _(dve):
            V = nc.vector
            chain = [0]

            def link(ins):
                chain[0] += 1
                ins.then_inc(sem("dve_chain"), 1)
                dve.wait_ge(sem("dve_chain"), chain[0])

            def note(ins):
                chain[0] += 1
                ins.then_inc(sem("dve_chain"), 1)

            def settle():
                dve.wait_ge(sem("dve_chain"), chain[0])

            def layer_norm(tag, src, dst, done=None):
                for t in range(QT):
                    note(V.bn_stats(st[:, t, :], src[:, t, :]))
                settle()
                for t in range(QT):
                    note(V.bn_aggr(mv[:, t, :], st[:, t, :]))
                settle()
                V.tensor_scalar(var_e[:, :], mv[:, :, 1], EPS, None, ALU.add).then_inc(sem(f"var_{tag}"), 1)
                dve.wait_ge(sem(f"std_{tag}"), 1)
                link(V.reciprocal(r_std[:, :], std[:, :]))
                for t in range(QT):
                    ins = V.tensor_scalar(dst[:, t, :], src[:, t, :], mv[:, t, 0:1], r_std[:, t:t + 1],
                                          ALU.subtract, ALU.mult)
                    ins.then_inc(sem(done), 1) if done else note(ins)
                settle()

            def split(f, parts, rest, w):
                link(V.tensor_tensor(rest[:, 0:w], f[:, 0:w], parts[:, 0, 0:w], ALU.subtract))
                link(V.tensor_copy(parts[:, 1, 0:w], rest[:, 0:w]))
                return V.tensor_tensor(parts[:, 2, 0:w], rest[:, 0:w], parts[:, 1, 0:w], ALU.subtract)

            def keys_values(l):
                dve.wait_ge(sem("v_ones"), 1)
                for c in range(NCH):
                    dve.wait_ge(sem(f"k_evac{l}"), 2 * (c + 1))
                    split(k_f[:, c % 2, :], k_st[:, c % 2, :, :], k_rest[:, c % 2, :], chunk_w[c]).then_inc(sem(f"k_split{l}"), 1)
                    dve.wait_ge(sem(f"v_proj{l}"), c + 1)
                    n = min(4, NFULL - 4 * c)

                    def add_bias(rows, t0, n, b0):
                        src = ps[0:rows, 2 + c % 2, b0 * P:(b0 + n) * P].rearrange("p (t h d) -> p t h d", t=n, h=H)
                        bias = b_row[0:rows, l, 0, :].rearrange("p (t h d) -> p t h d", t=1, h=H).broadcast_to([rows, n, H, HD])
                        return V.tensor_tensor(v_all[0:rows, t0:t0 + n, :, 0:HD], src, bias, ALU.add)

                    add_bias(P, 4 * c, n, 0).then_inc(sem(f"v_set{l}"), 1)
                    if c == NCH - 1:
                        add_bias(TAIL, NFULL, 1, n).then_inc(sem(f"v_set{l}"), 1)

            def queries(l):
                for half in range(2):
                    dve.wait_ge(sem(f"q_evac{l}"), 2 * (half + 1))
                    split(q_f[:, half, :], k_st[:, half, :, :], k_rest[:, half, :], HALF).then_inc(sem(f"q_split{l}"), 1)

            def max_tile(l, h, unit, t, slot):
                k = width(t)
                dve.wait_ge(sem(f"mx_filled{l}"), unit + 1)
                if t >= 2:
                    dve.wait_ge(sem(f"mx_done{l}"), unit - 1)
                    V.tensor_tensor(m_run[0:k, t % 2, :], flat(mx(slot)[0:k]), m_run[0:k, t % 2, :], ALU.max
                                    ).then_inc(sem(f"mx_done{l}"), 1)
                else:
                    if not (isinstance(h, int) and h == 0):
                        dve.wait_ge(sem(f"m_joined{l}"), h)
                    V.tensor_copy(m_run[:, t, :], flat(mx(slot))).then_inc(sem(f"mx_done{l}"), 1)

            def join(l, unit):
                dve.wait_ge(sem(f"mx_done{l}"), unit + 1)
                V.tensor_tensor(m_join, m_run[:, 0, :], m_run[:, 1, :], ALU.max).then_inc(sem(f"m_joined{l}"), 1)

            def reduce_max(l, h, unit, slot):
                dve.wait_ge(sem(f"mx_filled{l}"), unit + 1)
                V.tensor_reduce(m_neg[:, 0, :], flat(mx(slot)).rearrange("p (t k) -> p t k", k=P), AX.X, ALU.max,
                                negate=True).then_inc(sem(f"mx_done{l}"), 1)
                dve.wait_ge(sem(f"mx_done{l}"), unit + 1)
                V.tensor_copy(m_pad[:, :, MROW], m_neg[:, 0, :]).then_inc(sem(f"m_split{l}"), 1)
                dve.wait_ge(sem(f"m_split{l}"), h * 4 + 1)
                V.tensor_tensor(m_neg[:, 1, :], m_neg[:, 0, :], m_pad[:, :, MROW], ALU.subtract).then_inc(sem(f"m_split{l}"), 1)
                dve.wait_ge(sem(f"m_split{l}"), h * 4 + 2)
                V.tensor_copy(m_pad[:, :, MROW + 1], m_neg[:, 1, :]).then_inc(sem(f"m_split{l}"), 1)
                dve.wait_ge(sem(f"m_split{l}"), h * 4 + 3)
                V.tensor_tensor(m_pad[:, :, MROW + 2], m_neg[:, 1, :], m_pad[:, :, MROW + 1], ALU.subtract
                                ).then_inc(sem(f"m_split{l}"), 1)

            def set_rows(l, h, unit, slot):
                dve.wait_ge(sem(f"mx_filled{l}"), unit + 1)
                V.tensor_copy(q_ring[MROW:MROW + PARTS, bass.ds((h % RING) * TQ, TQ)],
                              ps[MROW:MROW + PARTS, 2 * slot, :].bitcast(BF16)).then_inc(sem(f"mx_done{l}"), 1)

            def o_norm(l, h, base, slot):
                o = mx(slot)[:, 0, 0:2 * P].rearrange("p (c g d) -> p c g d", c=2, g=QG)
                dve.wait_ge(sem(f"mx_filled{l}"), base + 1)
                V.reciprocal(r_den[:, :].rearrange("p (c g) -> p c g", c=2), o[:, :, :, HD]).then_inc(sem(f"r_den{l}"), 1)
                dve.wait_ge(sem(f"r_den{l}"), h + 1)
                V.tensor_tensor(o_all[:, :, bass.ds(h * HD, HD)].rearrange("p (g c) d -> p c g d", c=2), o[:, :, :, 0:HD],
                                r_den[:, :].rearrange("p (c g o) -> p c g o", c=2, o=1).broadcast_to([P, 2, QG, HD]),
                                ALU.mult).then_inc(sem(f"mx_done{l}"), 1)

            def one_unit(l, h, kind, unit, slot):
                if kind == "out":
                    o_norm(l, h, unit, slot)
                elif kind == "turn":
                    reduce_max(l, h + 1, unit, slot)
                elif kind == "rows":
                    set_rows(l, h + 1, unit, slot)
                else:
                    what, t = kind
                    max_tile(l, h + (1 if what == "max" else 2), unit, t, slot)
                    if t == NT - 1:
                        join(l, unit)

            def maxima(l):
                if l == 0:
                    dve.wait_ge(sem("mask_summed"), NFULL // MCH + 1)
                V.memset(o_raw[:, :], 1.0).then_inc(sem(f"o_raw{l}"), 1)
                for unit, kind in enumerate([("max", t) for t in range(NT)] + ENDING):
                    one_unit(l, -1, kind, unit, (unit + FIRST) % 2)
                with dve.Fori(0, LOOP) as h:
                    base = dve.snap(h * MXU)
                    for j, kind in enumerate(k for step in mx_steps(True) for k in step):
                        one_unit(l, h, kind, base + (FIRST + j), j % 2)
                for j, kind in enumerate(k for step in mx_steps(False) for k in step):
                    one_unit(l, H - 2, kind, LAST2 + j, j % 2)
                o_norm(l, H - 1, LAST, 0)
                dve.wait_ge(sem(f"mx_done{l}"), LAST + 1)
                o_norm(l, H, LAST + 1, 1)

            def attention_out(l):
                if l == 0:
                    dve.wait_ge(sem("mask_summed"), NFULL // MCH + 1)
                    link(V.tensor_scalar(m_sum[:, 0:5], m_sum[:, 0:5], -257.0 * MCH * TQ / 2, None, ALU.add))
                    link(V.tensor_scalar(m_sum[0:TAIL, 5:6], m_sum[0:TAIL, 5:6], -257.0 * TQ / 2, None, ALU.add))
                    link(V.tensor_reduce(m_tot[:, :], m_sum[:, 0:5], AX.X, ALU.add))
                    V.tensor_tensor(m_tot[0:TAIL, :], m_tot[0:TAIL, :], m_sum[0:TAIL, 5:6], ALU.add).then_inc(sem("mask_tot"), 1)
                    dve.wait_ge(sem("mask_all"), 1)
                    link(V.tensor_scalar(flag_f[:, :], ps[0:1, 7, 0:1], -0.5, None, ALU.is_lt))
                    V.tensor_copy(flag[:, :], flag_f[:, :]).then_inc(sem("flag_ready"), 1)
                dve.wait_ge(sem("g_tanh"), 1)
                dve.wait_ge(sem(f"o_proj{l}"), 2)
                bias = b_row[:, l, 1:2, :].broadcast_to([P, QT, C])
                V.tensor_tensor(x_ln[:, :, :], flat(ps[:, 2:4, :]).rearrange("p (t c) -> p t c", c=C), bias, ALU.add
                                ).then_inc(sem(f"att_added{l}"), 1)
                dve.wait_ge(sem(f"att_added{l}"), 1)
                link(V.scalar_tensor_tensor(out=flat(x_sb), in0=flat(x_ln), scalar=g_tanh[:, l:l + 1], in1=flat(x_sb),
                                            op0=ALU.mult, op1=ALU.add))

            def top_two(l):
                logit, prob, tmp, one1, gate, one2 = (ga[:, n, :, :] for n in range(6))

                def spread(n):
                    return gs[:, n, :].rearrange("p (t o) -> p t o", o=1).broadcast_to([P, QT, E])

                rank_b = rank[:, :].rearrange("p (o e) -> p o e", o=1).broadcast_to([P, QT, E])
                raw = ps[:, 7, 0:QT * E].rearrange("p (t e) -> p t e", e=E)
                dve.wait_ge(sem(f"logits{l}"), 1)
                dve.wait_ge(sem("rank"), E + 3)
                if l:
                    link(V.tensor_tensor(tmp, raw, br_row[:, :].rearrange("p (o e) -> p o e", o=1).broadcast_to([P, QT, E]), ALU.add))
                else:
                    link(V.tensor_copy(tmp, raw))
                link(V.tensor_reduce(gs[:, 0, :], tmp, AX.X, ALU.max))
                V.tensor_tensor(logit, tmp, spread(0), ALU.subtract).then_inc(sem(f"gate_in{l}"), 1)
                dve.wait_ge(sem(f"gate_exp{l}"), 1)
                pick, low = tmp, -3e38
                if l == 0:
                    link(V.tensor_reduce(gs[:, 1, :], prob, AX.X, ALU.add))
                    link(V.reciprocal(gs[:, 2, :], gs[:, 1, :]))
                    link(V.tensor_tensor(prob, prob, spread(2), ALU.mult))
                    pick, low = prob, -4.0

                def first_best(values, one, n):
                    link(V.tensor_reduce(gs[:, n, :], values, AX.X, ALU.max))
                    link(V.tensor_tensor(one, values, spread(n), ALU.is_equal))
                    link(V.tensor_tensor(one, one, rank_b, ALU.mult))
                    link(V.tensor_reduce(gs[:, n, :], one, AX.X, ALU.max))
                    link(V.tensor_tensor(one, rank_b, spread(n), ALU.is_equal))

                def value_at(one, n):
                    link(V.tensor_tensor(gate, prob, one, ALU.mult))
                    link(V.tensor_reduce(gs[:, n, :], gate, AX.X, ALU.add))

                first_best(pick, one1, 3)
                value_at(one1, 4)
                link(V.scalar_tensor_tensor(out=tmp, in0=one1, scalar=low, in1=pick, op0=ALU.mult, op1=ALU.add))
                first_best(tmp, one2, 3)
                value_at(one2, 5)
                link(V.tensor_tensor(gs[:, 0, :], gs[:, 4, :], gs[:, 5, :], ALU.add))
                if l == 0:
                    link(V.tensor_scalar(gs[:, 0, :], gs[:, 0, :], 1e-9, None, ALU.add))
                link(V.reciprocal(gs[:, 1, :], gs[:, 0, :]))
                link(V.tensor_tensor(tmp, one1, one2, ALU.add))
                link(V.tensor_tensor(tmp, tmp, prob, ALU.mult))
                V.tensor_tensor(gate, tmp, spread(1), ALU.mult).then_inc(sem(f"gates{l}"), 1)

            def gate_experts0():
                for u in range(E * 2 * 4):
                    e, half = u // 8, (u // 4) % 2
                    dve.wait_ge(sem("act_done0"), u + 1)
                    if u % 8 == 0:
                        dve.wait_ge(sem(f"gate_bc0_{e}"), 16)
                    if u >= 8:
                        dve.wait_ge(sem("down0"), u - 7)
                    V.tensor_tensor(hg_ring[:, u % 8, :], h_ring[:, u % 4, :], gate_bc[:, e, HALF * half:HALF * half + HALF],
                                    ALU.mult).then_inc(sem("gated0"), 1)

            def gate_experts1():
                for u in range(E * 2):
                    e, half = u // 2, u % 2
                    dve.wait_ge(sem("hidden1"), 4 * (u + 1))
                    if half == 0:
                        dve.wait_ge(sem(f"gate_bc1_{e}"), 16)
                    for t in range(2):
                        n = 2 * u + t
                        slot = 2 * (u % 2) + t
                        dve.wait_ge(sem("act_done1"), n + 1)
                        if n >= 8:
                            dve.wait_ge(sem("down1"), n - 7)
                        V.scalar_tensor_tensor(out=hg_ring[:, n % 8, :], in0=ps[:, 2 + t, :],
                                               scalar=b1_col[:, 1, e * 4 + 2 + t:e * 4 + 3 + t], in1=h_ring[:, slot, :],
                                               op0=ALU.add, op1=ALU.mult).then_inc(sem("glu1"), 1)
                        dve.wait_ge(sem("glu1"), n + 1)
                        V.tensor_tensor(hg_ring[:, n % 8, :], hg_ring[:, n % 8, :], gate_bc[:, e, HALF * half:HALF * half + HALF],
                                        ALU.mult).then_inc(sem("gated1"), 1)

            def ffn_out(l):
                dve.wait_ge(sem(f"turned_y{l}"), 2)
                y = flat(ps[:, 0:2, :])
                if l == 0:
                    link(V.tensor_tensor(flat(x_ln), y, flat(x_ln), ALU.add))
                    y = flat(x_ln)
                V.scalar_tensor_tensor(out=flat(x_sb), in0=y, scalar=g_tanh[:, 2 + l:3 + l], in1=flat(x_sb),
                                       op0=ALU.mult, op1=ALU.add).then_inc(sem(f"ffn_done{l}" if l == 0 else "x_final"), 1)

            def turn_mask():
                dve.wait_ge(sem("flag_ready"), 1)
                with dve.If(dve.value_load(flag[0:1, 0:1], min_val=0, max_val=1) > 0):
                    dve.wait_ge(sem("q_stored1"), 16 * 18)
                    V.memset(big[:, NFULL * TQ // 4:], 0.0).then_inc(sem("mask_tail"), 1)
                    for c in range(NFULL // MCH + 1):
                        dve.wait_ge(sem("mask_again"), 16 * (c + 1))
                        rows, n = (P, MCH) if c < NFULL // MCH else (TAIL, 1)
                        dve.wait_ge(sem("mask_tail"), 1)
                        V.tensor_scalar(mask_n[0:rows, c * MCH:c * MCH + n, :],
                                        mask_stage[0:rows, 0:n * TQ].rearrange("p (t q) -> p t q", t=n), -1.0, 1.0,
                                        ALU.mult, ALU.add, saturate=False).then_inc(sem("mask_turned"), 1)
                with dve.Else():
                    dve.nop()

            dve.wait_ge(sem("x_in"), 16)
            layer_norm("q0", x_sb, x_n, "xn_q0")
            keys_values(0)
            queries(0)
            maxima(0)
            attention_out(0)
            keys_values(1)
            dve.wait_ge(sem("small_in"), SMALL_IN)
            layer_norm("f0", x_sb, x_ln)
            layer_norm("g0", x_ln, x_n)
            link(V.tensor_tensor(x_n[:, :, :], x_n[:, :, :], gb_row[:, 0:1, :].broadcast_to([P, QT, C]), ALU.mult))
            V.tensor_tensor(x_n[:, :, :], x_n[:, :, :], gb_row[:, 1:2, :].broadcast_to([P, QT, C]), ALU.add).then_inc(sem("xn_f0"), 1)
            top_two(0)
            gate_experts0()
            ffn_out(0)
            dve.wait_ge(sem("ffn_done0"), 1)
            layer_norm("q1", x_sb, x_n, "xn_q1")
            queries(1)
            turn_mask()
            maxima(1)
            attention_out(1)
            layer_norm("f1", x_sb, x_n, "xn_f1")
            top_two(1)
            gate_experts1()
            ffn_out(1)

        @block.tensor
        def _(pe):
            def keys_values(l):
                pe.wait_ge(sem("att_w_in"), ATT_IN)
                pe.wait_ge(sem("ctx_in0"), 16)
                for c in range(NCH):
                    if c == 3:
                        pe.wait_ge(sem("ctx_in2048"), 16)
                    if c >= 2:
                        pe.wait_ge(sem(f"k_evac{l}"), 2 * (c - 1))
                    w = chunk_w[c]
                    pe.matmul(ps[:, c % 2, 0:w], w_att[:, l, 1, :], ctx_t[:, HALF * c:HALF * c + w],
                              start=True, stop=True).then_inc(sem(f"k_proj{l}"), 1)
                    if c == 0 and l:
                        pe.wait_ge(sem("att_added0"), 1)
                    if c >= 2:
                        pe.wait_ge(sem(f"v_set{l}"), c - 1)
                    for j in range(4):
                        t = 4 * c + j
                        if t < NT:
                            mm = pe.matmul(ps[0:width(t), 2 + c % 2, P * j:P * j + P], ctx_t[:, P * t:P * t + width(t)],
                                           w_att[:, l, 2, :], start=True, stop=True)
                    mm.then_inc(sem(f"v_proj{l}"), 1)

            def turn(tag, src, bank, after, n):
                pe.wait_ge(sem(after), n)
                for t in range(QT):
                    mm = pe.transpose(ps[:, bank + t // 4, P * (t % 4):P * (t % 4) + P], src(t), ident_f[:, :])
                    if t % 4 == 3:
                        mm.then_inc(sem(f"turned_{tag}"), 1)

            def queries(l):
                turn(f"q{l}", lambda t: x_n[:, t, :], 4, f"xn_q{l}", QT)
                pe.wait_ge(sem(f"copied_q{l}"), 1)
                for half in range(2):
                    pe.matmul(ps[:, 6 + half, :], w_att[:, l, 0, :], x_t[:, HALF * half:HALF * half + HALF],
                              start=True, stop=True).then_inc(sem(f"q_proj{l}"), 1)

            def key(koff, t, rows):
                return k_ring[0:rows, bass.ds(koff + P * t, width(t))]

            def query(qoff, half, rows):
                return q_ring[0:rows, bass.ds(qoff + HALF * half, HALF)]

            def score(dst, koff, qoff, t, half, rows, masked):
                k = width(t)
                if masked:
                    pe.matmul(dst[0:k], neg_i[:, 0:k], mask_n[:, t, HALF * half:HALF * half + HALF], start=True, stop=False)
                return pe.matmul(dst[0:k], key(koff, t, rows), query(qoff, half, rows), start=not masked, stop=True)

            def max_tile(l, unit, slot, koff, qoff, t, masked):
                if not (isinstance(unit, int) and unit < 2):
                    wait_apart(pe, "pe", sem(f"mx_done{l}"), unit - 1, masked or t == NT - 1)
                for half in range(2):
                    mm = score(mx(slot)[:, half, :], koff, qoff, t, half, ROWS_MAX, masked)
                mm.then_inc(sem(f"mx_filled{l}"), 1)

            def turn_max(l, h, unit, slot):
                pe.wait_ge(sem(f"mx_done{l}"), unit - 1)
                pe.wait_ge(sem(f"m_joined{l}"), h + 1)
                for t in range(QT):
                    mm = pe.transpose(mx(slot)[:, t // 4, P * (t % 4):P * (t % 4) + P], m_join[:, P * t:P * t + P], ident_f[:, :])
                mm.then_inc(sem(f"mx_filled{l}"), 1)

            def turn_rows(l, h, unit, slot):
                pe.wait_ge(sem(f"mx_done{l}"), unit - 1)
                pe.wait_ge(sem(f"m_split{l}"), h * 4 + 4)
                rows = ps[:, 2 * slot, :].bitcast(BF16)
                for t in range(QT):
                    mm = pe.transpose(rows[:, P * t:P * t + P], m_pad[:, t, :], ident_b[:, :])
                mm.then_inc(sem(f"mx_filled{l}"), 1)

            def turn_out(l, h, unit, slot):
                pe.wait_ge(sem(f"mx_done{l}"), unit - 1)
                pe.wait_ge(sem(f"o_raw{l}"), h + 1)
                for c in range(2):
                    mm = pe.transpose(mx(slot)[:, 0, P * c:P * c + P], o_raw[:, P * c:P * c + P], ident_f[:, :])
                mm.then_inc(sem(f"mx_filled{l}"), 1)

            def exp_unit(l, h, koff, qoff, u, masked):
                t, half = u // 2, u % 2
                wait_apart(pe, "pe", sem(f"exp_done{l}"), h * (2 * NT) + (u + 1), masked or t == NT - 1)
                score(ps[:, 4 + u % EXB, :], koff, qoff, t, half, ROWS_EXP, masked).then_inc(sem(f"scored{l}"), 1)

            def weigh(l, h, t):
                k = width(t)
                if t == 0:
                    pe.wait_ge(sem(f"o_raw{l}"), h + 1)
                for n, (t0, _) in enumerate(V_CHUNKS):
                    if t == t0:
                        pe.wait_ge(sem(f"v_head{l}"), h * len(V_CHUNKS) + (n + 1))
                wait_apart(pe, "pe", sem(f"exp_done{l}"), h * (2 * NT) + (2 * t + 2 + EXB), t == NT - 1)
                for g in range(QG):
                    mm = pe.matmul(ps[32 * g:32 * g + VW, 7, 0:QGW], v_head[0:k, t, :], probs[0:k, t % PSLOTS, QGW * g:QGW * g + QGW],
                                   start=(t == 0), stop=(t == NT - 1))
                mm.then_inc(sem(f"pv_done{l}"), 1)

            def place(n, w):
                return n % RING * w if isinstance(n, int) else pe.snap((n % RING) * w)

            def one_unit(l, h, kind, unit, slot, at, masked):
                if kind == "out":
                    turn_out(l, h, unit, slot)
                elif kind == "turn":
                    turn_max(l, h + 1, unit, slot)
                elif kind == "rows":
                    turn_rows(l, h + 1, unit, slot)
                else:
                    what, t = kind
                    koff, qoff = at[0 if what == "max" else 1]
                    max_tile(l, unit, slot, koff, qoff, t, masked)

            def head(l, h, base, masked, steps):
                at = [(place(h + n, TK), place(h + n, TQ)) for n in range(3)]
                wait_apart(pe, "pe", sem(f"mx_done{l}"), base - AFTER_ROWS if not isinstance(h, int) or h < H - 1 else base, masked)
                j = 0
                for s, tiles in enumerate(STEP_TILES):
                    scores = [u for t in tiles for u in (2 * t, 2 * t + 1)]
                    units = list(steps[s])
                    exp_unit(l, h, *at[0], scores.pop(0), masked)
                    while scores or units:
                        if scores:
                            exp_unit(l, h, *at[0], scores.pop(0), masked)
                        if units:
                            if units[0] == ("next", 0):
                                pe.wait_ge(sem(f"head_in{l}"), h * 64 + 192)
                            one_unit(l, h, units.pop(0), base + j, j % 2, at[1:], masked)
                            j += 1
                    for t in STEP_TILES[s - 1] if s else ():
                        weigh(l, h, t)
                for t in STEP_TILES[-1]:
                    weigh(l, h, t)

            def attention(l, masked):
                pe.wait_ge(sem(f"head_in{l}"), 64)
                pe.matmul(ps[:, 7, 0:QGW], zeros_b[:, 0:P], zeros_b[:, 0:QGW], start=True, stop=True).then_inc(sem(f"pv_done{l}"), 1)
                for unit, kind in enumerate([("max", t) for t in range(NT)] + ENDING):
                    if kind == ("next", 0):
                        pe.wait_ge(sem(f"head_in{l}"), 128)
                    one_unit(l, -1, kind, unit, (unit + FIRST) % 2, [(0, 0), (TK, TQ)], masked)
                with pe.Fori(0, LOOP) as h:
                    head(l, h, pe.snap(h * MXU + FIRST), masked, mx_steps(True))
                head(l, H - 2, LAST2, masked, mx_steps(False))
                head(l, H - 1, LAST, masked, [["out"] if s == 1 else [] for s in range(NSTEP)])
                turn_out(l, H, LAST + 1, 1)

            def attention_out(l):
                turn(f"o{l}", lambda t: o_all[:, t, HD:HD + C], 0, f"mx_done{l}", LAST + 2)
                pe.wait_ge(sem(f"copied_o{l}"), 1)
                for t in range(QT):
                    mm = pe.matmul(ps[:, 2 + t // 4, P * (t % 4):P * (t % 4) + P], x_t[:, P * t:P * t + P], w_att[:, l, 3, :],
                                   start=True, stop=True)
                    if t % 4 == 3:
                        mm.then_inc(sem(f"o_proj{l}"), 1)

            def gating(l):
                turn(f"f{l}", lambda t: x_n[:, t, :], 0, f"xn_f{l}", (1, QT)[l])
                pe.wait_ge(sem(f"copied_f{l}"), 1)
                pe.wait_ge(sem("small_in"), SMALL_IN)
                for t in range(QT):
                    mm = pe.matmul(ps[:, 7, E * t:E * t + E], x_t[:, P * t:P * t + P], w_gate[:, l, :], start=True, stop=True)
                mm.then_inc(sem(f"logits{l}"), 1)

            def turn_gates(l):
                pe.wait_ge(sem(f"gates{l}"), 1)
                for t in range(QT):
                    mm = pe.transpose(ps[0:E, 2 + t // 4, P * (t % 4):P * (t % 4) + P], ga[:, 4, t, :], ident_f[:, :])
                mm.then_inc(sem(f"gate_turned{l}"), 1)

            def experts(l):
                w1, w2, nd = (w1_0, w2_0, 4) if l == 0 else (w1_1, w2_1, 2)
                turn_gates(l)
                pe.wait_ge(sem(f"gate_t{l}"), 1)
                pe.wait_ge(sem(f"experts_in{l}"), 32)
                for half in range(2):
                    pe.matmul(ps[:, 4 + half, :], b2_sb[:, l, :], gate_t[:, HALF * half:HALF * half + HALF],
                              start=True, stop=False)

                def up(u):
                    e, half = u // 2, u % 2
                    for t in range(4):
                        n = 4 * u + t
                        if u >= 1 and l == 0:
                            pe.wait_ge(sem("act_done0"), n - 3)
                        if u >= 1 and l == 1 and t < 2:
                            pe.wait_ge(sem("act_done1"), 2 * (u - 1) + t + 1)
                        if u >= 1 and l == 1 and t >= 2:
                            pe.wait_ge(sem("glu1"), 2 * (u - 1) + t - 1)
                        pe.matmul(ps[:, t, :], w1[:, e, P * t:P * t + P], x_t[:, HALF * half:HALF * half + HALF],
                                  start=True, stop=True).then_inc(sem(f"hidden{l}"), 1)

                def down(u):
                    e, half = u // 2, u % 2
                    for t in range(nd):
                        n = nd * u + t
                        pe.wait_ge(sem(f"gated{l}"), n + 1)
                        mm = pe.matmul(ps[:, 4 + half, :], w2[:, e, t, :], hg_ring[:, n % 8, :],
                                       start=False, stop=(e == E - 1 and t == nd - 1))
                        mm.then_inc(sem(f"down{l}"), 1)
                    return mm

                for u in range(2 * E):
                    up(u)
                    if u:
                        down(u - 1)
                down(2 * E - 1)

            def y_out(l):
                pe.wait_ge(sem(f"y_t{l}"), 1)
                for t in range(QT):
                    mm = pe.transpose(ps[:, t // 4, P * (t % 4):P * (t % 4) + P], y_t[:, P * t:P * t + P], ident_f[:, :])
                    if t % 4 == 3:
                        mm.then_inc(sem(f"turned_y{l}"), 1)

            pe.wait_ge(sem("ident"), 2)
            pe.wait_ge(sem("v_ones"), 1)
            keys_values(0)
            queries(0)
            attention(0, False)
            pe.wait_ge(sem("mask_tot"), 1)
            pe.wait_ge(sem("rank"), E + 3)
            pe.matmul(ps[0:1, 7, 0:1], m_tot[:, :], ones_f[:, :], start=True, stop=True).then_inc(sem("mask_all"), 1)
            attention_out(0)
            keys_values(1)
            gating(0)
            experts(0)
            y_out(0)
            queries(1)
            pe.wait_ge(sem("flag_ready"), 1)
            with pe.If(pe.value_load(flag[0:1, 0:1], min_val=0, max_val=1) > 0):
                pe.wait_ge(sem("mask_turned"), NFULL // MCH + 1)
                attention(1, True)
            with pe.Else():
                attention(1, False)
            attention_out(1)
            gating(1)
            experts(1)
            y_out(1)


def kernel(x, ctx_1024, mask_Bx1xSxS2_bf1, g_xattn, g_ffn, **w):
    import concourse.bacc as bacc
    from concourse.bass_utils import run_bass_kernel_spmd

    nc = bacc.Bacc("TRN2", target_bir_lowering=False, num_devices=1)
    lay = np.ascontiguousarray
    arrays = {
        "x": lay(np.asarray(x).reshape(TQ, C)),
        "ctx_t": lay(np.asarray(ctx_1024).reshape(TK, C).T),
        "mask_t": lay(np.asarray(mask_Bx1xSxS2_bf1).reshape(TQ, TK).view(np.uint8).T),
        "g_xattn": lay(g_xattn), "g_ffn": lay(g_ffn),
        "gamma": lay(w["L0_ffn_gamma"]), "beta": lay(w["L0_ffn_beta"]), "br": lay(w["L1_ffn_br"]),
        "w_gate0": lay(np.asarray(w["L0_ffn_Wg"]).T), "w_gate1": lay(w["L1_ffn_Wr"]),
    }
    for l in range(2):
        for n in "qkvo":
            arrays[f"w{n}{l}"] = lay(np.asarray(w[f"L{l}_xattn_W{n}"]).T)
            bias = np.asarray(w[f"L{l}_xattn_b{n}"])
            arrays[f"b{n}{l}"] = lay(bias.reshape(C, 1) if n in "qk" else bias)
        arrays[f"w1_{l}"] = lay(w[f"L{l}_ffn_W1"])
        arrays[f"w2_{l}"] = lay(w[f"L{l}_ffn_W2"])
        arrays[f"b1_{l}"] = lay(np.asarray(w[f"L{l}_ffn_b1"]).reshape(E * FF // P, P).T)
        arrays[f"b2_{l}"] = lay(w[f"L{l}_ffn_b2"])
    arrays = {f"in_{n}": v for n, v in arrays.items()}
    args = {n[3:]: nc.dram_tensor(n, v.shape, mybir.dt.from_np(v.dtype), kind="ExternalInput").ap() for n, v in arrays.items()}
    out = nc.dram_tensor("out", [TQ, C], F32, kind="ExternalOutput").ap()
    block_kernel(nc, args, out)
    r = run_bass_kernel_spmd(nc, [arrays], core_ids=[0])
    return r.results[0]["out"].reshape(1, TQ, C)
```

```python
from contextlib import ExitStack

import concourse.bass as bass
import numpy as np
from concourse import mybir

F32 = mybir.dt.float32
BF16 = mybir.dt.bfloat16
F8 = mybir.dt.float8e5
U8 = mybir.dt.uint8
U16 = mybir.dt.uint16
I32 = mybir.dt.int32
ALU = mybir.AluOpType
ACT = mybir.ActivationFunctionType
AX = mybir.AxisListType

P = 128
C = 128
H = 16
HD = C // H
TQ = 1024
TK = 6404
QT = TQ // P
NFULL = TK // P
TAIL = TK - NFULL * P
NT = NFULL + 1
HALF = 512
E = 8
FF = 512
EPS = 1e-5
SCALE = float(HD) ** -0.5
MASKED = -1e20

PARTS = 3
KR = PARTS * HD
QKR = PARTS * KR
MROW = 96
ROWS_MAX = MROW
ROWS_EXP = MROW + PARTS
VW = HD + 1
QG = 4
QGW = TQ // QG
RING = 3
STEP = 2
NSTEP = -(-NT // STEP)
PSLOTS = 5
EXB = 3
V_CHUNKS = [(0, 12), (12, 24), (24, 36), (36, NT)]
AHEAD = 8
ENDING = [[("next", 0)], ["turn", ("next", 1)], [("next", 2), ("next", 3)], ["rows", ("next", 4), ("next", 5)],
          [("next", 6)], [("next", 7)]]
ENDING_UNITS = sum(ENDING, [])
AFTER_ROWS = len(ENDING_UNITS) - 1 - ENDING_UNITS.index("rows")
STEP_OUT = 1
STEPS_OF_3 = (5, 10, 15)
MXU = NT + 3


def mx_steps(ahead):
    steps, t = [], AHEAD
    for s in range(NSTEP - len(ENDING)):
        n = 3 if s in STEPS_OF_3 else 2
        steps.append([("max", t + i) for i in range(n)] + ["out"] * (s == STEP_OUT))
        t += n
    assert t == NT
    return steps + [[u for u in step if ahead or isinstance(u, str)] for step in ENDING]


P_FIVES = NT - 4 * (-NT % 5)


def p_slot(t):
    return t % 5 if t < P_FIVES else (t - P_FIVES) % 4


def p_before(t):
    return max(u for u in range(-NT, t) if p_slot(u % NT) == p_slot(t))


assert MXU % 2 == 0 and AHEAD % 2 == 0 and 2 * NT % EXB == 0
assert P_FIVES % 5 == 0 and (NT - P_FIVES) % 4 == 0 and all(t - p_before(t) >= 4 for t in range(NT))


MCH = 5


def width(t):
    return P if t < NFULL else TAIL


def block_kernel(nc, a, out):
    with ExitStack() as ctx:
        def sb(name, shape, dt=F32):
            return ctx.enter_context(nc.sbuf_tensor(name, shape, dt))

        sems = {}

        def sem(name):
            if name not in sems:
                sems[name] = ctx.enter_context(nc.semaphore(name))
            return sems[name]

        k_parts = [nc.dram_tensor(f"k_parts{l}", [C, PARTS, TK], BF16, kind="Internal").ap() for l in range(2)]
        q_rows = [nc.dram_tensor(f"q_rows{l}", [H, PARTS, HD, PARTS, TQ], BF16, kind="Internal").ap() for l in range(2)]
        gate_rows = [nc.dram_tensor(f"gate_rows{l}", [E, TQ], F32, kind="Internal").ap() for l in range(2)]

        ps = ctx.enter_context(nc.psum_tensor("ps", [P, 8, HALF], F32))

        def flat3(t):
            return t[:, :, :].rearrange("p a b -> p (a b)")

        ctx_t = sb("ctx_t", [P, TK])
        w1_1 = ctx_t[:, 0:E * FF].rearrange("p (e f) -> p e f", e=E)
        w2_1 = ctx_t[:, E * FF:E * FF + E * 2 * C].rearrange("p (e t d) -> p e t d", e=E, t=2)
        k_ring = sb("k_ring", [P, RING * TK], BF16)
        q_ring = sb("q_ring", [P, RING * TQ], BF16)
        gate_bc = k_ring[:, 0:E * TQ * 2].bitcast(F32).rearrange("p (e q) -> p e q", e=E)
        v_all = sb("v_all", [P, NT, H, VW])
        v_head = sb("v_head", [P, NT, VW])
        probs = sb("probs", [P, PSLOTS + 1, TQ])
        m_join = probs[:, PSLOTS, :]
        mask_stage = [flat3(probs)[:, n * MCH * TQ // 4:(n + 1) * MCH * TQ // 4].bitcast(U8) for n in range(2)]
        mask_junk = flat3(probs)[:, 3 * TQ:3 * TQ + MCH * TQ // 4].bitcast(BF16)
        h_ring = probs[:, 0:2, :].rearrange("p a (b c) -> p (a b) c", b=2)
        hg_ring = probs[:, 2:6, :].rearrange("p a (b c) -> p (a b) c", b=2)
        big = sb("big", [P, NT * TQ // 4])
        w1_0 = big[:, 0:E * FF].rearrange("p (e f) -> p e f", e=E)
        w2_0 = big[:, E * FF:2 * E * FF].rearrange("p (e t d) -> p e t d", e=E, t=4)
        mask_n = big[:, :].bitcast(F8).rearrange("p (t q) -> p t q", t=NT)
        spare = big[:, 2 * E * FF:]
        k_f = spare[:, 0:2 * HALF].rearrange("p (a w) -> p a w", a=2)
        k_rest = spare[:, 2 * HALF:4 * HALF].rearrange("p (a w) -> p a w", a=2)
        k_st = spare[:, 4 * HALF:7 * HALF].bitcast(BF16).rearrange("p (a b w) -> p a b w", a=2, b=PARTS)
        gate_t = spare[0:E, 7 * HALF:7 * HALF + TQ]
        q_f = k_f
        m_run = sb("m_run", [P, 2, TQ])
        x_t = m_run[:, 0, :]
        y_t = m_run[:, 1, :]
        x_n = y_t.rearrange("p (t c) -> p t c", c=C)
        x_sb = sb("x_sb", [P, QT, C])
        o_all = sb("o_all", [P, QT, (H + 1) * HD])
        x_ln = flat3(o_all)[:, 0:QT * C].rearrange("p (t c) -> p t c", c=C)
        o_raw = sb("o_raw", [P, QGW])
        m_neg = sb("m_neg", [P, 2, QT])
        m_pad = sb("m_pad", [P, QT, P], BF16)
        r_den = sb("r_den", [P, QT])
        w_att = sb("w_att", [P, 2, 4, C])
        b_col = sb("b_col", [P, 2, 2])
        b_row = sb("b_row", [P, 2, 2, C])
        gb_row = sb("gb_row", [P, 2, C])
        w_gate = sb("w_gate", [P, 2, E])
        br_row = sb("br_row", [P, E])
        b1_col = sb("b1_col", [P, 2, E * 4])
        b2_sb = sb("b2_sb", [E, 2, C])
        g_raw = sb("g_raw", [P, 4])
        g_tanh = sb("g_tanh", [P, 4])
        ident_f = sb("ident_f", [P, P])
        ident_b = sb("ident_b", [P, P], BF16)
        neg_i = sb("neg_i", [P, P], BF16)
        ones_f = sb("ones_f", [P, 1])
        ones_b = sb("ones_b", [P, QGW], BF16)
        rank = sb("rank", [P, E])
        st = sb("st", [P, QT, 6])
        mv = sb("mv", [P, QT, 2])
        var_e = sb("var_e", [P, QT])
        std = sb("std", [P, QT])
        r_std = sb("r_std", [P, QT])
        ga = sb("ga", [P, 6, QT, E])
        gs = sb("gs", [P, 6, QT])
        m_sum = sb("m_sum", [P, NFULL // MCH + 1])
        m_tot = sb("m_tot", [P, 1])
        flag_f = sb("flag_f", [1, 1])
        flag = sb("flag", [1, 1], I32)

        def mx(slot):
            return ps[:, 2 * slot:2 * slot + 2, :]

        def flat(ap):
            return ap.rearrange("p a b -> p (a b)")

        NCH = -(-TK // HALF)
        chunk_w = [min(HALF, TK - HALF * c) for c in range(NCH)]
        CTX_CHUNKS = [(0, 2 * HALF), (2 * HALF, 6 * HALF), (6 * HALF, TK)]
        ATT_IN, SMALL_IN = 8 * 16, 16 * 9
        FIRST = NT + len(ENDING_UNITS)
        LOOP = H - 2
        LAST2 = FIRST + MXU * LOOP
        LAST = LAST2 + MXU - AHEAD
        MX_OUT = sum(len(u) for u in mx_steps(True)[:STEP_OUT + 1])


        def wait_apart(eng, name, s, value, apart=True):
            eng.wait_ge(s, value)
            if apart and not isinstance(value, int):
                eng.sem_inc(sem(f"{name}_apart"), 1)

        block = ctx.enter_context(nc.Block())

        @block.sync
        def _(sp):
            def setup():
                def attention_weights(l):
                    for n, w in enumerate("qkvo"):
                        sp.dma_start(w_att[:, l, n, :], a[f"w{w}{l}"]).then_inc(sem(f"att_w_in{l}"), 16)
                    for n, w in enumerate("qk"):
                        sp.dma_start(b_col[:, l, n:n + 1], a[f"b{w}{l}"]).then_inc(sem(f"att_w_in{l}"), 16)
                    for n, w in enumerate("vo"):
                        sp.dma_start(b_row[:, l, n, :], a[f"b{w}{l}"].partition_broadcast(P)).then_inc(sem(f"att_w_in{l}"), 16)

                attention_weights(0)
                for c0, c1 in CTX_CHUNKS:
                    sp.dma_start(ctx_t[:, c0:c1], a["ctx_t"][:, c0:c1]).then_inc(sem(f"ctx_in{c0}"), 16)
                attention_weights(1)
                sp.dma_start(g_raw[:, 0:2], a["g_xattn"].partition_broadcast(P)).then_inc(sem("g_in"), 16)
                sp.dma_start(g_raw[:, 2:4], a["g_ffn"].partition_broadcast(P)).then_inc(sem("g_in"), 16)
                for l in range(2):
                    sp.dma_start(w_gate[:, l, :], a[f"w_gate{l}"]).then_inc(sem("small_in"), 16)
                    sp.dma_start(b1_col[:, l, :], a[f"b1_{l}"]).then_inc(sem("small_in"), 16)
                    sp.dma_start(b2_sb[:, l, :], a[f"b2_{l}"]).then_inc(sem("small_in"), 16)
                for n, w in enumerate(("gamma", "beta")):
                    sp.dma_start(gb_row[:, n, :], a[w].partition_broadcast(P)).then_inc(sem("small_in"), 16)
                sp.dma_start(br_row[:, :], a["br"].partition_broadcast(P)).then_inc(sem("small_in"), 16)
                sp.dma_start(w1_0, a["w1_0"].rearrange("e d f -> d e f")).then_inc(sem("experts_in0"), 16)
                sp.dma_start(w2_0.rearrange("p e t d -> p (e t) d"),
                             a["w2_0"].rearrange("e (t f) d -> f (e t) d", f=P)).then_inc(sem("experts_in0"), 16)

            def store_k(l):
                for c in range(NCH):
                    sp.wait_ge(sem(f"k_split{l}"), c + 1)
                    sp.dma_start(k_parts[l][:, :, HALF * c:HALF * c + chunk_w[c]],
                                 k_st[:, c % 2, :, 0:chunk_w[c]]).then_inc(sem(f"k_stored{l}_{c % 2}"), 16)

            def store_q(l):
                for half in range(2):
                    sp.wait_ge(sem(f"q_split{l}"), half + 1)
                    for b in range(PARTS):
                        for d in range(PARTS):
                            sp.dma_start(q_rows[l].rearrange("h b d a w -> b a h d w")[b, d][:, :, HALF * half:HALF * half + HALF],
                                         k_st[:, half, b, :]).then_inc(sem(f"q_stored{l}"), 16)

            def check_mask():
                for c in range(NFULL // MCH):
                    if c > 1:
                        sp.wait_ge(sem("mask_summed"), c - 1)
                    sp.dma_start(mask_stage[c % 2].rearrange("p (t q) -> p t q", q=TQ),
                                 a["mask_t"][c * MCH * P:(c + 1) * MCH * P, :].rearrange("(t p) q -> p t q", p=P)
                                 ).then_inc(sem(f"mask_in{c % 2}"), 16)
                sp.wait_ge(sem("mask_summed"), NFULL // MCH - 1)
                sp.dma_start(mask_stage[0][0:TAIL, 0:TQ], a["mask_t"][NFULL * P:TK, :]).then_inc(sem("mask_in0"), 16)

            def build_mask():
                sp.wait_ge(sem("flag_ready"), 1)
                sp.wait_ge(sem("ffn_done0"), 1)
                with sp.If(sp.value_load(flag[0:1, 0:1], min_val=0, max_val=1) > 0):
                    for c in range(NFULL // MCH):
                        if c:
                            sp.wait_ge(sem("mask_turned"), c)
                        sp.dma_start(mask_stage[0].rearrange("p (t q) -> p t q", q=TQ),
                                     a["mask_t"][c * MCH * P:(c + 1) * MCH * P, :].rearrange("(t p) q -> p t q", p=P)
                                     ).then_inc(sem("mask_again"), 16)
                    sp.wait_ge(sem("mask_turned"), NFULL // MCH)
                    sp.dma_start(mask_stage[0][0:TAIL, 0:TQ], a["mask_t"][NFULL * P:TK, :]).then_inc(sem("mask_again"), 16)
                with sp.Else():
                    sp.nop()

            def load_head(l, h):
                def place(w):
                    return h % RING * w if isinstance(h, int) else sp.snap((h % RING) * w)

                koff, qoff = place(TK), place(TQ)
                if not isinstance(h, int):
                    wait_apart(sp, "sp", sem(f"scored{l}"), h * (2 * NT) - (RING - 1) * 2 * NT)
                for b in range(PARTS):
                    sp.dma_start(k_ring[b * KR:(b + 1) * KR, bass.ds(koff, TK)],
                                 k_parts[l][bass.ds(h * HD, HD)].rearrange("d a w -> (d a) w")
                                 ).then_inc(sem(f"head_in{l}"), 16)
                sp.dma_start(q_ring[0:QKR, bass.ds(qoff, TQ)],
                             q_rows[l][bass.ds(h, 1)].rearrange("h b d a w -> (h b d a) w")).then_inc(sem(f"head_in{l}"), 16)

            def load_heads(l):
                sp.wait_ge(sem("ring_set"), 3 + 2 * l)
                sp.wait_ge(sem(f"k_stored{l}_0"), 16 * (-(-NCH // 2)))
                sp.wait_ge(sem(f"k_stored{l}_1"), 16 * (NCH // 2))
                sp.wait_ge(sem(f"q_stored{l}"), 16 * 18)
                for h in range(RING):
                    load_head(l, h)
                    sp.wait_ge(sem(f"head_in{l}"), 64 * (h + 1))
                if l == 0:
                    check_mask()
                with sp.Fori(RING, H) as h:
                    load_head(l, h)
                    wait_apart(sp, "sp", sem(f"head_in{l}"), 64 * h + 64)

            def spread_gates(l):
                sp.wait_ge(sem(f"gate_t{l}"), 1)
                sp.dma_start(gate_rows[l], gate_t[:, :]).then_inc(sem(f"gate_out{l}"), 16)
                sp.wait_ge(sem(f"gate_out{l}"), 16)
                for e in range(E):
                    sp.dma_start(gate_bc[:, e, :], gate_rows[l][e:e + 1, :].rearrange("e q -> (e q)").partition_broadcast(P)
                                 ).then_inc(sem(f"gate_bc{l}_{e}"), 16)

            sp.dma_start(x_sb[:, :, :], a["x"].rearrange("(t p) c -> p t c", p=P)).then_inc(sem("x_in"), 16)
            setup()
            store_k(0)
            store_q(0)
            load_heads(0)
            store_k(1)
            sp.wait_ge(sem("v_proj1"), NCH)
            sp.wait_ge(sem("k_proj1"), NCH)
            sp.dma_start(w1_1, a["w1_1"].rearrange("e d f -> d e f")).then_inc(sem("experts_in1"), 16)
            sp.dma_start(w2_1.rearrange("p e t d -> p (e t) d"),
                         a["w2_1"].rearrange("e (t f) d -> f (e t) d", f=P)).then_inc(sem("experts_in1"), 16)
            spread_gates(0)
            store_q(1)
            build_mask()
            load_heads(1)
            spread_gates(1)
            sp.wait_ge(sem("x_final"), 1)
            sp.dma_start(out.rearrange("(t p) c -> p t c", p=P), x_sb[:, :, :]).then_inc(sem("out_stored"), 16)
            sp.wait_ge(sem("out_stored"), 16)

        @block.gpsimd
        def _(pool):
            chain = [0]

            def link(ins):
                chain[0] += 1
                ins.then_inc(sem("pool_chain"), 1)
                pool.wait_ge(sem("pool_chain"), chain[0])

            def constants():
                link(nc.gpsimd.memset(ident_f[:, :], 0.0))
                nc.gpsimd.affine_select(out=ident_f[:, :], in_=ident_f[:, :], compare_op=ALU.not_equal, fill=1.0,
                                        base=0, pattern=[[-1, P]], channel_multiplier=1).then_inc(sem("ident"), 1)
                pool.wait_ge(sem("ident"), 1)
                nc.gpsimd.tensor_copy(ident_b[:, :], ident_f[:, :]).then_inc(sem("ident"), 1)
                nc.gpsimd.memset(ones_b[:, :], 1.0).then_inc(sem("ones_set"), 1)
                for e in range(E):
                    nc.gpsimd.memset(rank[:, e:e + 1], float(E - e)).then_inc(sem("rank"), 1)
                nc.gpsimd.memset(ones_f[:, :], 1.0).then_inc(sem("rank"), 1)
                nc.gpsimd.memset(m_pad[:, :, :], 0.0).then_inc(sem("rank"), 1)
                nc.gpsimd.tensor_scalar(neg_i[:, :], ident_f[:, :], MASKED, 0.0, ALU.mult, ALU.add).then_inc(sem("rank"), 1)
                pool.wait_ge(sem("rank"), E + 3)

            def v_chunk(l, h, n):
                t0, t1 = V_CHUNKS[n]
                nc.gpsimd.tensor_copy(v_head[:, t0:t1, :], v_all[:, t0:t1, bass.ds(h, 1), :].rearrange("p t o d -> p t (o d)")
                                      ).then_inc(sem(f"v_head{l}"), 1)

            def v_heads(l):
                pool.wait_ge(sem(f"v_set{l}"), NCH + 1)
                if l == 0:
                    pool.wait_ge(sem("v_init"), 2)
                for n in range(len(V_CHUNKS)):
                    v_chunk(l, 0, n)
                with pool.Fori(1, H) as h:
                    for n, (_, t1) in enumerate(V_CHUNKS):
                        pool.wait_ge(sem(f"pv_done{l}"), h * NT + t1)
                        v_chunk(l, h, n)

            constants()
            v_heads(0)
            pool.wait_ge(sem("pv_done0"), (H + 1) * NT)
            v_heads(1)

        @block.scalar
        def _(act):
            A = nc.scalar.activation

            def project_k():
                for c in range(NCH):
                    w = chunk_w[c]
                    act.wait_ge(sem("k_proj0"), c + 1)
                    if c >= 2:
                        act.wait_ge(sem("k_split0"), c - 1)
                        act.wait_ge(sem(f"k_stored0_{c % 2}"), 16 * (c // 2))
                    A(k_f[:, c % 2, 0:w], ps[:, c % 2, 0:w], ACT.Identity, bias=b_col[:, 0, 1:2]).then_inc(sem("k_evac0"), 1)
                    A(k_st[:, c % 2, 0, 0:w], ps[:, c % 2, 0:w], ACT.Identity, bias=b_col[:, 0, 1:2]).then_inc(sem("k_evac0"), 1)

            def set_v(c):
                n = min(4, NFULL - 4 * c)
                act.wait_ge(sem("v_proj0"), c + 1)
                bank = ps[:, 4 + c % 4, :].rearrange("p (t h d) -> p t h d", t=4, h=H)
                A(v_all[:, 4 * c:4 * c + n, :, 0:HD], bank[:, 0:n], ACT.Identity).then_inc(sem("v_set0"), 1)
                if c == NCH - 1:
                    act.wait_ge(sem("v_init"), 2)
                    A(v_all[0:TAIL, NFULL:NT, :, 0:HD], bank[0:TAIL, n:n + 1], ACT.Identity).then_inc(sem("v_set0"), 1)

            def std_of(tag):
                act.wait_ge(sem(f"var_{tag}"), 1)
                A(std[:, :], var_e[:, :], ACT.Sqrt).then_inc(sem(f"std_{tag}"), 1)

            def turned(tag, bank, dst):
                act.wait_ge(sem(f"turned_{tag}"), 2)
                A(dst, flat(ps[:, bank:bank + 2, :]), ACT.Identity).then_inc(sem(f"copied_{tag}"), 1)

            def project_q(l):
                turned(f"q{l}", 4, x_t)
                act.wait_ge(sem(f"k_split{l}"), NCH)
                act.wait_ge(sem(f"k_stored{l}_0"), 16 * (-(-NCH // 2)))
                act.wait_ge(sem(f"k_stored{l}_1"), 16 * (NCH // 2))
                for half in range(2):
                    act.wait_ge(sem(f"q_proj{l}"), half + 1)
                    A(q_f[:, half, :], ps[:, 6 + half, :], ACT.Identity, bias=b_col[:, l, 0:1]).then_inc(sem(f"q_evac{l}"), 1)
                    A(k_st[:, half, 0, :], ps[:, 6 + half, :], ACT.Identity, bias=b_col[:, l, 0:1]).then_inc(sem(f"q_evac{l}"), 1)

            def sum_mask(c):
                act.wait_ge(sem(f"mask_in{c % 2}"), 16 * (c // 2 + 1))
                rows, n = (P, MCH * TQ // 2) if c < NFULL // MCH else (TAIL, TQ // 2)
                if c:
                    act.wait_ge(sem("mask_summed"), c)
                A(mask_junk[0:rows, 0:n], mask_stage[c % 2][0:rows, 0:2 * n].bitcast(U16), ACT.Copy,
                  accum_out=m_sum[0:rows, c:c + 1]).then_inc(sem("mask_summed"), 1)

            def evacuate(l, h, out_unit):
                act.wait_ge(sem(f"pv_done{l}"), h * NT + NT)
                act.wait_ge(sem(f"mx_filled{l}"), out_unit)
                A(o_raw[:, :], ps[:, 7, 0:QGW], ACT.Identity).then_inc(sem(f"o_raw{l}"), 1)

            def exp_head(l, h, out_unit):
                for t in range(NT):
                    k = width(t)
                    act.wait_ge(sem(f"pv_done{l}"), h * NT + (NT + p_before(t) + 1))
                    for half in range(2):
                        u = 2 * t + half
                        act.wait_ge(sem(f"scored{l}"), h * (2 * NT) + (u + 1))
                        A(probs[0:k, p_slot(t), HALF * half:HALF * half + HALF], ps[0:k, 4 + u % EXB, :], ACT.Exp,
                          scale=SCALE).then_inc(sem(f"exp_done{l}"), 1)
                    if t == STEP - 1:
                        evacuate(l, h, out_unit)

            def exp_all(l):
                act.nop().then_inc(sem(f"exp_done{l}"), EXB)
                with act.Fori(0, LOOP) as h:
                    exp_head(l, h, h * MXU + (FIRST + MX_OUT - MXU))
                exp_head(l, H - 2, LAST2 + MX_OUT - MXU)
                exp_head(l, H - 1, LAST2 + MX_OUT)
                evacuate(l, H, LAST + 1)

            def gates(l):
                act.wait_ge(sem(f"gate_in{l}"), 1)
                A(ga[:, 1, :, :], ga[:, 0, :, :], ACT.Exp).then_inc(sem(f"gate_exp{l}"), 1)

            def gates_turned(l):
                act.wait_ge(sem(f"gate_turned{l}"), 1)
                A(gate_t[:, :], flat(ps[0:E, 2:4, :]), ACT.Identity).then_inc(sem(f"gate_t{l}"), 1)

            def experts0():
                for u in range(E * 2 * 4):
                    e, t = u // 8, u % 4
                    act.wait_ge(sem("hidden0"), u + 1)
                    if u >= 4:
                        act.wait_ge(sem("gated0"), u - 3)
                    A(h_ring[:, u % 4, :], ps[:, u % 4, :], ACT.Gelu_apprx_tanh,
                      bias=b1_col[:, 0, e * 4 + t:e * 4 + t + 1]).then_inc(sem("act_done0"), 1)

            def experts1():
                for u in range(E * 2):
                    e = u // 2
                    act.wait_ge(sem("hidden1"), 4 * u + 2)
                    for t in range(2):
                        if u >= 2:
                            act.wait_ge(sem("gated1"), 2 * (u - 2) + t + 1)
                        A(h_ring[:, 2 * (u % 2) + t, :], ps[:, t, :], ACT.Silu,
                          bias=b1_col[:, 1, e * 4 + t:e * 4 + t + 1]).then_inc(sem("act_done1"), 1)

            def y_out(l):
                act.wait_ge(sem(f"down{l}"), 2 * E * (4, 2)[l])
                A(y_t, flat(ps[:, 4:6, :]), ACT.Identity).then_inc(sem(f"y_t{l}"), 1)

            act.wait_ge(sem("g_in"), 32)
            A(g_tanh[:, :], g_raw[:, :], ACT.Tanh).then_inc(sem("g_tanh"), 1)
            act.wait_ge(sem("att_w_in0"), ATT_IN)
            std_of("q0")
            project_k()
            project_q(0)
            for c in range(NCH):
                set_v(c)
                if c < NFULL // MCH + 1:
                    sum_mask(c)
            act.wait_ge(sem("mask_summed"), NFULL // MCH + 1)
            exp_all(0)
            turned("o0", 0, x_t)
            std_of("f0")
            std_of("g0")
            turned("f0", 0, x_t)
            gates(0)
            gates_turned(0)
            experts0()
            y_out(0)
            std_of("q1")
            project_q(1)
            exp_all(1)
            turned("o1", 0, x_t)
            std_of("f1")
            turned("f1", 0, x_t)
            gates(1)
            gates_turned(1)
            experts1()
            y_out(1)

        @block.vector
        def _(dve):
            V = nc.vector
            chain = [0]

            def link(ins):
                chain[0] += 1
                ins.then_inc(sem("dve_chain"), 1)
                dve.wait_ge(sem("dve_chain"), chain[0])

            def note(ins):
                chain[0] += 1
                ins.then_inc(sem("dve_chain"), 1)

            def settle():
                dve.wait_ge(sem("dve_chain"), chain[0])

            def layer_norm(tag, src, dst, done=None):
                for t in range(QT):
                    note(V.bn_stats(st[:, t, :], src[:, t, :]))
                settle()
                for t in range(QT):
                    note(V.bn_aggr(mv[:, t, :], st[:, t, :]))
                settle()
                V.tensor_scalar(var_e[:, :], mv[:, :, 1], EPS, None, ALU.add).then_inc(sem(f"var_{tag}"), 1)
                dve.wait_ge(sem(f"std_{tag}"), 1)
                link(V.reciprocal(r_std[:, :], std[:, :]))
                for t in range(QT):
                    ins = V.tensor_scalar(dst[:, t, :], src[:, t, :], mv[:, t, 0:1], r_std[:, t:t + 1],
                                          ALU.subtract, ALU.mult)
                    ins.then_inc(sem(done), 1) if done else note(ins)
                settle()

            def split(f, parts, rest, w):
                link(V.tensor_tensor(rest[:, 0:w], f[:, 0:w], parts[:, 0, 0:w], ALU.subtract))
                link(V.tensor_copy(parts[:, 1, 0:w], rest[:, 0:w]))
                return V.tensor_tensor(parts[:, 2, 0:w], rest[:, 0:w], parts[:, 1, 0:w], ALU.subtract)

            def split_keys():
                for c in range(NCH):
                    dve.wait_ge(sem("k_evac0"), 2 * (c + 1))
                    split(k_f[:, c % 2, :], k_st[:, c % 2, :, :], k_rest[:, c % 2, :], chunk_w[c]).then_inc(sem("k_split0"), 1)

            def next_keys_values():
                dve.wait_ge(sem("v_head0"), H * len(V_CHUNKS))
                dve.wait_ge(sem("q_stored0"), 16 * 18)
                dve.wait_ge(sem("att_w_in1"), ATT_IN)
                for c in range(NCH):
                    w = chunk_w[c]
                    dve.wait_ge(sem("k_proj1"), c + 1)
                    if c >= 2:
                        dve.wait_ge(sem(f"k_stored1_{c % 2}"), 16 * (c // 2))
                    for dst in (k_f[:, c % 2, 0:w], k_st[:, c % 2, 0, 0:w]):
                        ins = V.tensor_scalar(dst, ps[:, c % 2, 0:w], b_col[:, 1, 1:2], None, ALU.add)
                        ins.then_inc(sem("k_evac1"), 1)
                    dve.wait_ge(sem("k_evac1"), 2 * (c + 1))
                    split(k_f[:, c % 2, :], k_st[:, c % 2, :, :], k_rest[:, c % 2, :], w).then_inc(sem("k_split1"), 1)
                    n = min(4, NFULL - 4 * c)
                    dve.wait_ge(sem("v_proj1"), c + 1)
                    bank = ps[:, 2 + c % 2, :].rearrange("p (t h d) -> p t h d", t=4, h=H)
                    V.tensor_copy(v_all[:, 4 * c:4 * c + n, :, 0:HD], bank[:, 0:n]).then_inc(sem("v_set1"), 1)
                    if c == NCH - 1:
                        V.tensor_copy(v_all[0:TAIL, NFULL:NT, :, 0:HD], bank[0:TAIL, n:n + 1]).then_inc(sem("v_set1"), 1)

            def set_ring(l):
                if l == 0:
                    V.memset(q_ring[2 * 32:MROW, :], 0.0).then_inc(sem("ring_set"), 1)
                else:
                    dve.wait_ge(sem("gated0"), 2 * E * 4)
                V.memset(k_ring[2 * 32:MROW, :], 0.0).then_inc(sem("ring_set"), 1)
                V.memset(k_ring[MROW:P, :], 1.0).then_inc(sem("ring_set"), 1)

            def queries(l):
                for half in range(2):
                    dve.wait_ge(sem(f"q_evac{l}"), 2 * (half + 1))
                    split(q_f[:, half, :], k_st[:, half, :, :], k_rest[:, half, :], HALF).then_inc(sem(f"q_split{l}"), 1)

            def max_tile(l, h, unit, t, slot):
                k = width(t)
                dve.wait_ge(sem(f"mx_filled{l}"), unit + 1)
                if t >= 2:
                    dve.wait_ge(sem(f"mx_done{l}"), unit - 1)
                    V.tensor_tensor(m_run[0:k, t % 2, :], flat(mx(slot)[0:k]), m_run[0:k, t % 2, :], ALU.max
                                    ).then_inc(sem(f"mx_done{l}"), 1)
                else:
                    if not (isinstance(h, int) and h == 0):
                        dve.wait_ge(sem(f"m_joined{l}"), h)
                    V.tensor_copy(m_run[:, t, :], flat(mx(slot))).then_inc(sem(f"mx_done{l}"), 1)

            def join(l, unit):
                dve.wait_ge(sem(f"mx_done{l}"), unit + 1)
                V.tensor_tensor(m_join, m_run[:, 0, :], m_run[:, 1, :], ALU.max).then_inc(sem(f"m_joined{l}"), 1)

            def reduce_max(l, h, unit, slot):
                dve.wait_ge(sem(f"mx_filled{l}"), unit + 1)
                V.tensor_reduce(m_neg[:, 0, :], flat(mx(slot)).rearrange("p (t k) -> p t k", k=P), AX.X, ALU.max,
                                negate=True).then_inc(sem(f"mx_done{l}"), 1)
                dve.wait_ge(sem(f"mx_done{l}"), unit + 1)
                V.tensor_copy(m_pad[:, :, MROW], m_neg[:, 0, :]).then_inc(sem(f"m_split{l}"), 1)
                dve.wait_ge(sem(f"m_split{l}"), h * 4 + 1)
                V.tensor_tensor(m_neg[:, 1, :], m_neg[:, 0, :], m_pad[:, :, MROW], ALU.subtract).then_inc(sem(f"m_split{l}"), 1)
                dve.wait_ge(sem(f"m_split{l}"), h * 4 + 2)
                V.tensor_copy(m_pad[:, :, MROW + 1], m_neg[:, 1, :]).then_inc(sem(f"m_split{l}"), 1)
                dve.wait_ge(sem(f"m_split{l}"), h * 4 + 3)
                V.tensor_tensor(m_pad[:, :, MROW + 2], m_neg[:, 1, :], m_pad[:, :, MROW + 1], ALU.subtract
                                ).then_inc(sem(f"m_split{l}"), 1)

            def set_rows(l, h, unit, slot):
                dve.wait_ge(sem(f"mx_filled{l}"), unit + 1)
                V.tensor_copy(q_ring[MROW:MROW + PARTS, bass.ds((h % RING) * TQ, TQ)],
                              ps[MROW:MROW + PARTS, 2 * slot, :].bitcast(BF16)).then_inc(sem(f"mx_done{l}"), 1)

            def o_norm(l, h, base, slot):
                o = mx(slot)[:, 0, 0:2 * P].rearrange("p (c g d) -> p c g d", c=2, g=QG)
                dve.wait_ge(sem(f"mx_filled{l}"), base + 1)
                V.reciprocal(r_den[:, :].rearrange("p (c g) -> p c g", c=2), o[:, :, :, HD]).then_inc(sem(f"r_den{l}"), 1)
                dve.wait_ge(sem(f"r_den{l}"), h + 1)
                V.tensor_tensor(o_all[:, :, bass.ds(h * HD, HD)].rearrange("p (g c) d -> p c g d", c=2), o[:, :, :, 0:HD],
                                r_den[:, :].rearrange("p (c g o) -> p c g o", c=2, o=1).broadcast_to([P, 2, QG, HD]),
                                ALU.mult).then_inc(sem(f"mx_done{l}"), 1)

            def one_unit(l, h, kind, unit, slot):
                if kind == "out":
                    o_norm(l, h, unit, slot)
                elif kind == "turn":
                    reduce_max(l, h + 1, unit, slot)
                elif kind == "rows":
                    set_rows(l, h + 1, unit, slot)
                else:
                    what, t = kind
                    max_tile(l, h + (1 if what == "max" else 2), unit, t, slot)
                    if t == NT - 1:
                        join(l, unit)

            def maxima(l):
                dve.wait_ge(sem("rank"), E + 3)
                for unit, kind in enumerate([("max", t) for t in range(NT)] + ENDING_UNITS):
                    one_unit(l, -1, kind, unit, (unit + FIRST) % 2)
                with dve.Fori(0, LOOP) as h:
                    base = dve.snap(h * MXU)
                    for j, kind in enumerate(k for step in mx_steps(True) for k in step):
                        one_unit(l, h, kind, base + (FIRST + j), j % 2)
                for j, kind in enumerate(k for step in mx_steps(False) for k in step):
                    one_unit(l, H - 2, kind, LAST2 + j, j % 2)
                o_norm(l, H - 1, LAST, 0)
                dve.wait_ge(sem(f"mx_done{l}"), LAST + 1)
                if l == 0:
                    next_keys_values()
                o_norm(l, H, LAST + 1, 1)
                dve.wait_ge(sem(f"mx_done{l}"), LAST + 2)
                V.tensor_tensor(o_all[:, :, HD:HD + C], o_all[:, :, HD:HD + C], b_row[:, l, 0:1, :].broadcast_to([P, QT, C]),
                                ALU.add).then_inc(sem(f"o_biased{l}"), 1)

            def attention_out(l):
                if l == 0:
                    dve.wait_ge(sem("mask_summed"), NFULL // MCH + 1)
                    n = NFULL // MCH
                    link(V.tensor_scalar(m_sum[:, 0:n], m_sum[:, 0:n], -257.0 * MCH * TQ / 2, None, ALU.add))
                    link(V.tensor_scalar(m_sum[0:TAIL, n:n + 1], m_sum[0:TAIL, n:n + 1], -257.0 * TQ / 2, None, ALU.add))
                    link(V.tensor_reduce(m_tot[:, :], m_sum[:, 0:n], AX.X, ALU.add))
                    V.tensor_tensor(m_tot[0:TAIL, :], m_tot[0:TAIL, :], m_sum[0:TAIL, n:n + 1], ALU.add).then_inc(sem("mask_tot"), 1)
                    dve.wait_ge(sem("mask_all"), 1)
                    link(V.tensor_scalar(flag_f[:, :], ps[0:1, 7, 0:1], -0.5, None, ALU.is_lt))
                    V.tensor_copy(flag[:, :], flag_f[:, :]).then_inc(sem("flag_ready"), 1)
                dve.wait_ge(sem("g_tanh"), 1)
                dve.wait_ge(sem(f"o_proj{l}"), 2)
                bias = b_row[:, l, 1:2, :].broadcast_to([P, QT, C])
                V.tensor_tensor(x_ln[:, :, :], flat(ps[:, 2:4, :]).rearrange("p (t c) -> p t c", c=C), bias, ALU.add
                                ).then_inc(sem(f"att_added{l}"), 1)
                dve.wait_ge(sem(f"att_added{l}"), 1)
                link(V.scalar_tensor_tensor(out=flat(x_sb), in0=flat(x_ln), scalar=g_tanh[:, l:l + 1], in1=flat(x_sb),
                                            op0=ALU.mult, op1=ALU.add))

            def top_two(l):
                logit, prob, tmp, one1, gate, one2 = (ga[:, n, :, :] for n in range(6))

                def spread(n):
                    return gs[:, n, :].rearrange("p (t o) -> p t o", o=1).broadcast_to([P, QT, E])

                rank_b = rank[:, :].rearrange("p (o e) -> p o e", o=1).broadcast_to([P, QT, E])
                raw = ps[:, 7, 0:QT * E].rearrange("p (t e) -> p t e", e=E)
                dve.wait_ge(sem(f"logits{l}"), 1)
                dve.wait_ge(sem("rank"), E + 3)
                if l:
                    link(V.tensor_tensor(tmp, raw, br_row[:, :].rearrange("p (o e) -> p o e", o=1).broadcast_to([P, QT, E]), ALU.add))
                else:
                    link(V.tensor_copy(tmp, raw))
                link(V.tensor_reduce(gs[:, 0, :], tmp, AX.X, ALU.max))
                V.tensor_tensor(logit, tmp, spread(0), ALU.subtract).then_inc(sem(f"gate_in{l}"), 1)
                dve.wait_ge(sem(f"gate_exp{l}"), 1)
                pick, low = tmp, -3e38
                if l == 0:
                    link(V.tensor_reduce(gs[:, 1, :], prob, AX.X, ALU.add))
                    link(V.reciprocal(gs[:, 2, :], gs[:, 1, :]))
                    link(V.tensor_tensor(prob, prob, spread(2), ALU.mult))
                    pick, low = prob, -4.0

                def first_best(values, one, n):
                    link(V.tensor_reduce(gs[:, n, :], values, AX.X, ALU.max))
                    link(V.tensor_tensor(one, values, spread(n), ALU.is_equal))
                    link(V.tensor_tensor(one, one, rank_b, ALU.mult))
                    link(V.tensor_reduce(gs[:, n, :], one, AX.X, ALU.max))
                    link(V.tensor_tensor(one, rank_b, spread(n), ALU.is_equal))

                def value_at(one, n):
                    link(V.tensor_tensor(gate, prob, one, ALU.mult))
                    link(V.tensor_reduce(gs[:, n, :], gate, AX.X, ALU.add))

                first_best(pick, one1, 3)
                value_at(one1, 4)
                link(V.scalar_tensor_tensor(out=tmp, in0=one1, scalar=low, in1=pick, op0=ALU.mult, op1=ALU.add))
                first_best(tmp, one2, 3)
                value_at(one2, 5)
                link(V.tensor_tensor(gs[:, 0, :], gs[:, 4, :], gs[:, 5, :], ALU.add))
                if l == 0:
                    link(V.tensor_scalar(gs[:, 0, :], gs[:, 0, :], 1e-9, None, ALU.add))
                link(V.reciprocal(gs[:, 1, :], gs[:, 0, :]))
                link(V.tensor_tensor(tmp, one1, one2, ALU.add))
                link(V.tensor_tensor(tmp, tmp, prob, ALU.mult))
                V.tensor_tensor(gate, tmp, spread(1), ALU.mult).then_inc(sem(f"gates{l}"), 1)

            def gate_experts0():
                for u in range(E * 2 * 4):
                    e, half = u // 8, (u // 4) % 2
                    dve.wait_ge(sem("act_done0"), u + 1)
                    if u % 8 == 0:
                        dve.wait_ge(sem(f"gate_bc0_{e}"), 16)
                    if u >= 8:
                        dve.wait_ge(sem("down0"), u - 7)
                    V.tensor_tensor(hg_ring[:, u % 8, :], h_ring[:, u % 4, :], gate_bc[:, e, HALF * half:HALF * half + HALF],
                                    ALU.mult).then_inc(sem("gated0"), 1)

            def gate_experts1():
                for u in range(E * 2):
                    e, half = u // 2, u % 2
                    dve.wait_ge(sem("hidden1"), 4 * (u + 1))
                    if half == 0:
                        dve.wait_ge(sem(f"gate_bc1_{e}"), 16)
                    for t in range(2):
                        n = 2 * u + t
                        slot = 2 * (u % 2) + t
                        dve.wait_ge(sem("act_done1"), n + 1)
                        if n >= 8:
                            dve.wait_ge(sem("down1"), n - 7)
                        V.scalar_tensor_tensor(out=hg_ring[:, n % 8, :], in0=ps[:, 2 + t, :],
                                               scalar=b1_col[:, 1, e * 4 + 2 + t:e * 4 + 3 + t], in1=h_ring[:, slot, :],
                                               op0=ALU.add, op1=ALU.mult).then_inc(sem("glu1"), 1)
                        dve.wait_ge(sem("glu1"), n + 1)
                        V.tensor_tensor(hg_ring[:, n % 8, :], hg_ring[:, n % 8, :], gate_bc[:, e, HALF * half:HALF * half + HALF],
                                        ALU.mult).then_inc(sem("gated1"), 1)

            def ffn_out(l):
                dve.wait_ge(sem(f"turned_y{l}"), 2)
                y = flat(ps[:, 0:2, :])
                if l == 0:
                    link(V.tensor_tensor(flat(x_ln), y, flat(x_ln), ALU.add))
                    y = flat(x_ln)
                V.scalar_tensor_tensor(out=flat(x_sb), in0=y, scalar=g_tanh[:, 2 + l:3 + l], in1=flat(x_sb),
                                       op0=ALU.mult, op1=ALU.add).then_inc(sem(f"ffn_done{l}" if l == 0 else "x_final"), 1)

            def turn_mask():
                dve.wait_ge(sem("flag_ready"), 1)
                with dve.If(dve.value_load(flag[0:1, 0:1], min_val=0, max_val=1) > 0):
                    dve.wait_ge(sem("q_stored1"), 16 * 18)
                    V.memset(big[:, NFULL * TQ // 4:], 0.0).then_inc(sem("mask_tail"), 1)
                    for c in range(NFULL // MCH + 1):
                        dve.wait_ge(sem("mask_again"), 16 * (c + 1))
                        rows, n = (P, MCH) if c < NFULL // MCH else (TAIL, 1)
                        dve.wait_ge(sem("mask_tail"), 1)
                        V.tensor_scalar(mask_n[0:rows, c * MCH:c * MCH + n, :],
                                        mask_stage[0][0:rows, 0:n * TQ].rearrange("p (t q) -> p t q", t=n), -1.0, 1.0,
                                        ALU.mult, ALU.add, saturate=False).then_inc(sem("mask_turned"), 1)
                with dve.Else():
                    dve.nop()

            V.memset(v_all[:, :, :, HD:VW], 1.0).then_inc(sem("v_init"), 1)
            V.memset(v_all[:, NFULL:NT, :, 0:HD], 0.0).then_inc(sem("v_init"), 1)
            set_ring(0)
            dve.wait_ge(sem("x_in"), 16)
            layer_norm("q0", x_sb, x_n, "xn_q0")
            split_keys()
            queries(0)
            maxima(0)
            attention_out(0)
            dve.wait_ge(sem("small_in"), SMALL_IN)
            layer_norm("f0", x_sb, x_ln)
            layer_norm("g0", x_ln, x_n)
            link(V.tensor_tensor(x_n[:, :, :], x_n[:, :, :], gb_row[:, 0:1, :].broadcast_to([P, QT, C]), ALU.mult))
            V.tensor_tensor(x_n[:, :, :], x_n[:, :, :], gb_row[:, 1:2, :].broadcast_to([P, QT, C]), ALU.add).then_inc(sem("xn_f0"), 1)
            top_two(0)
            gate_experts0()
            set_ring(1)
            ffn_out(0)
            dve.wait_ge(sem("ffn_done0"), 1)
            layer_norm("q1", x_sb, x_n, "xn_q1")
            queries(1)
            turn_mask()
            maxima(1)
            attention_out(1)
            layer_norm("f1", x_sb, x_n, "xn_f1")
            top_two(1)
            gate_experts1()
            ffn_out(1)

        @block.tensor
        def _(pe):
            def keys(l, c):
                w = chunk_w[c]
                if l == 0:
                    for c0, _ in CTX_CHUNKS:
                        if c * HALF == c0:
                            pe.wait_ge(sem(f"ctx_in{c0}"), 16)
                if c >= 2:
                    pe.wait_ge(sem(f"k_evac{l}"), 2 * (c - 1))
                pe.matmul(ps[:, c % 2, 0:w], w_att[:, l, 1, :], ctx_t[:, HALF * c:HALF * c + w],
                          start=True, stop=True).then_inc(sem(f"k_proj{l}"), 1)

            def values(l, c, bank, banks):
                if c >= banks:
                    pe.wait_ge(sem(f"v_set{l}"), c - banks + 1)
                for t in range(4 * c, min(4 * c + 4, NT)):
                    mm = pe.matmul(ps[0:width(t), bank + c % banks, P * (t % 4):P * (t % 4) + P],
                                   ctx_t[:, P * t:P * t + width(t)], w_att[:, l, 2, :], start=True, stop=True)
                mm.then_inc(sem(f"v_proj{l}"), 1)

            def turn(tag, src, bank, after, n):
                pe.wait_ge(sem(after), n)
                for t in range(QT):
                    mm = pe.transpose(ps[:, bank + t // 4, P * (t % 4):P * (t % 4) + P], src(t), ident_f[:, :])
                    if t % 4 == 3:
                        mm.then_inc(sem(f"turned_{tag}"), 1)

            def queries(l):
                turn(f"q{l}", lambda t: x_n[:, t, :], 4, f"xn_q{l}", QT)
                pe.wait_ge(sem(f"copied_q{l}"), 1)
                for half in range(2):
                    pe.matmul(ps[:, 6 + half, :], w_att[:, l, 0, :], x_t[:, HALF * half:HALF * half + HALF],
                              start=True, stop=True).then_inc(sem(f"q_proj{l}"), 1)

            def key(koff, t, rows):
                return k_ring[0:rows, bass.ds(koff + P * t, width(t))]

            def query(qoff, half, rows):
                return q_ring[0:rows, bass.ds(qoff + HALF * half, HALF)]

            def score(dst, koff, qoff, t, half, rows, masked):
                k = width(t)
                if masked:
                    pe.matmul(dst[0:k], neg_i[:, 0:k], mask_n[:, t, HALF * half:HALF * half + HALF], start=True, stop=False)
                return pe.matmul(dst[0:k], key(koff, t, rows), query(qoff, half, rows), start=not masked, stop=True)

            def max_tile(l, unit, slot, koff, qoff, t, masked):
                if not (isinstance(unit, int) and unit < 2):
                    wait_apart(pe, "pe", sem(f"mx_done{l}"), unit - 1, masked or t == NT - 1)
                for half in range(2):
                    mm = score(mx(slot)[:, half, :], koff, qoff, t, half, ROWS_MAX, masked)
                mm.then_inc(sem(f"mx_filled{l}"), 1)

            def turn_max(l, h, unit, slot):
                pe.wait_ge(sem(f"mx_done{l}"), unit - 1)
                pe.wait_ge(sem(f"m_joined{l}"), h + 1)
                for t in range(QT):
                    mm = pe.transpose(mx(slot)[:, t // 4, P * (t % 4):P * (t % 4) + P], m_join[:, P * t:P * t + P], ident_f[:, :])
                mm.then_inc(sem(f"mx_filled{l}"), 1)

            def turn_rows(l, h, unit, slot):
                pe.wait_ge(sem(f"mx_done{l}"), unit - 1)
                pe.wait_ge(sem(f"m_split{l}"), h * 4 + 4)
                rows = ps[:, 2 * slot, :].bitcast(BF16)
                for t in range(QT):
                    mm = pe.transpose(rows[:, P * t:P * t + P], m_pad[:, t, :], ident_b[:, :])
                mm.then_inc(sem(f"mx_filled{l}"), 1)

            def turn_out(l, h, unit, slot):
                pe.wait_ge(sem(f"mx_done{l}"), unit - 1)
                pe.wait_ge(sem(f"o_raw{l}"), h + 1)
                for c in range(2):
                    mm = pe.transpose(mx(slot)[:, 0, P * c:P * c + P], o_raw[:, P * c:P * c + P], ident_f[:, :])
                mm.then_inc(sem(f"mx_filled{l}"), 1)

            def exp_unit(l, h, koff, qoff, u, masked):
                t, half = u // 2, u % 2
                wait_apart(pe, "pe", sem(f"exp_done{l}"), h * (2 * NT) + (u + 1), masked or t == NT - 1)
                score(ps[:, 4 + u % EXB, :], koff, qoff, t, half, ROWS_EXP, masked).then_inc(sem(f"scored{l}"), 1)

            def weigh(l, h, t):
                k = width(t)
                if t == 0:
                    pe.wait_ge(sem(f"o_raw{l}"), h + 1)
                for n, (t0, _) in enumerate(V_CHUNKS):
                    if t == t0:
                        pe.wait_ge(sem(f"v_head{l}"), h * len(V_CHUNKS) + (n + 1))
                wait_apart(pe, "pe", sem(f"exp_done{l}"), h * (2 * NT) + (2 * t + 2 + EXB), t == NT - 1)
                for g in range(QG):
                    mm = pe.matmul(ps[32 * g:32 * g + VW, 7, 0:QGW], v_head[0:k, t, :], probs[0:k, p_slot(t), QGW * g:QGW * g + QGW],
                                   start=(t == 0), stop=(t == NT - 1))
                mm.then_inc(sem(f"pv_done{l}"), 1)

            def place(n, w):
                return n % RING * w if isinstance(n, int) else pe.snap((n % RING) * w)

            def one_unit(l, h, kind, unit, slot, at, masked):
                if kind == "out":
                    turn_out(l, h, unit, slot)
                elif kind == "turn":
                    turn_max(l, h + 1, unit, slot)
                elif kind == "rows":
                    turn_rows(l, h + 1, unit, slot)
                else:
                    what, t = kind
                    koff, qoff = at[0 if what == "max" else 1]
                    max_tile(l, unit, slot, koff, qoff, t, masked)

            def head(l, h, base, masked, steps, keys_values=False):
                at = [(place(h + n, TK), place(h + n, TQ)) for n in range(3)]
                wait_apart(pe, "pe", sem(f"mx_done{l}"), base - AFTER_ROWS if not isinstance(h, int) or h < H - 1 else base, masked)
                j = 0
                for s in range(NSTEP):
                    scores = list(range(2 * STEP * s, min(2 * STEP * (s + 1), 2 * NT)))
                    if ("next", 0) in steps[s]:
                        pe.wait_ge(sem(f"head_in{l}"), h * 64 + 192)
                    exp_unit(l, h, *at[0], scores.pop(0), masked)
                    for kind in (steps[s] + [None] * 2)[:2]:
                        if scores:
                            exp_unit(l, h, *at[0], scores.pop(0), masked)
                        if kind:
                            one_unit(l, h, kind, base + j, j % 2, at[1:], masked)
                            j += 1
                    if keys_values and (s == 1 or s and s % 2 == 0):
                        c = s // 2
                        if c == 0:
                            pe.wait_ge(sem("att_w_in1"), ATT_IN)
                            pe.wait_ge(sem("mx_done0"), LAST + 1)
                        keys(1, c)
                        values(1, c, 2, 2)
                    for u in scores:
                        exp_unit(l, h, *at[0], u, masked)
                    for t in range(STEP * (s - 1), STEP * s) if s else ():
                        weigh(l, h, t)
                    for kind in steps[s][2:]:
                        one_unit(l, h, kind, base + j, j % 2, at[1:], masked)
                        j += 1
                for t in range(STEP * (NSTEP - 1), NT):
                    weigh(l, h, t)

            def attention(l, masked):
                pe.wait_ge(sem(f"head_in{l}"), 64)
                for unit, kind in enumerate([("max", t) for t in range(NT)] + ENDING_UNITS):
                    if kind == ("next", 0):
                        pe.wait_ge(sem(f"head_in{l}"), 128)
                    one_unit(l, -1, kind, unit, (unit + FIRST) % 2, [(0, 0), (TK, TQ)], masked)
                    if l == 0 and unit % 4 == 3 and unit // 4 < NCH:
                        values(0, unit // 4, 4, 4)
                if l == 0:
                    pe.wait_ge(sem("v_set0"), NCH + 1)
                pe.matmul(ps[:, 7, 0:QGW], ones_b[:, 0:P], ones_b[:, 0:QGW], start=True, stop=True).then_inc(sem(f"pv_done{l}"), NT)
                with pe.Fori(0, LOOP) as h:
                    head(l, h, pe.snap(h * MXU + FIRST), masked, mx_steps(True))
                head(l, H - 2, LAST2, masked, mx_steps(False))
                head(l, H - 1, LAST, masked, [["out"] if s == 1 else [] for s in range(NSTEP)], l == 0)
                if l == 0:
                    pe.wait_ge(sem("v_set1"), NCH + 1)
                turn_out(l, H, LAST + 1, 1)

            def attention_out(l):
                turn(f"o{l}", lambda t: o_all[:, t, HD:HD + C], 0, f"o_biased{l}", 1)
                pe.wait_ge(sem(f"copied_o{l}"), 1)
                for t in range(QT):
                    mm = pe.matmul(ps[:, 2 + t // 4, P * (t % 4):P * (t % 4) + P], x_t[:, P * t:P * t + P], w_att[:, l, 3, :],
                                   start=True, stop=True)
                    if t % 4 == 3:
                        mm.then_inc(sem(f"o_proj{l}"), 1)

            def gating(l):
                turn(f"f{l}", lambda t: x_n[:, t, :], 0, f"xn_f{l}", (1, QT)[l])
                pe.wait_ge(sem(f"copied_f{l}"), 1)
                pe.wait_ge(sem("small_in"), SMALL_IN)
                for t in range(QT):
                    mm = pe.matmul(ps[:, 7, E * t:E * t + E], x_t[:, P * t:P * t + P], w_gate[:, l, :], start=True, stop=True)
                mm.then_inc(sem(f"logits{l}"), 1)

            def turn_gates(l):
                pe.wait_ge(sem(f"gates{l}"), 1)
                for t in range(QT):
                    mm = pe.transpose(ps[0:E, 2 + t // 4, P * (t % 4):P * (t % 4) + P], ga[:, 4, t, :], ident_f[:, :])
                mm.then_inc(sem(f"gate_turned{l}"), 1)

            def experts(l):
                w1, w2, nd = (w1_0, w2_0, 4) if l == 0 else (w1_1, w2_1, 2)
                turn_gates(l)
                pe.wait_ge(sem(f"gate_t{l}"), 1)
                pe.wait_ge(sem(f"experts_in{l}"), 32)
                for half in range(2):
                    pe.matmul(ps[:, 4 + half, :], b2_sb[:, l, :], gate_t[:, HALF * half:HALF * half + HALF],
                              start=True, stop=False)

                def up(u):
                    e, half = u // 2, u % 2
                    for t in range(4):
                        n = 4 * u + t
                        if u >= 1 and l == 0:
                            pe.wait_ge(sem("act_done0"), n - 3)
                        if u >= 1 and l == 1 and t < 2:
                            pe.wait_ge(sem("act_done1"), 2 * (u - 1) + t + 1)
                        if u >= 1 and l == 1 and t >= 2:
                            pe.wait_ge(sem("glu1"), 2 * (u - 1) + t - 1)
                        pe.matmul(ps[:, t, :], w1[:, e, P * t:P * t + P], x_t[:, HALF * half:HALF * half + HALF],
                                  start=True, stop=True).then_inc(sem(f"hidden{l}"), 1)

                def down(u):
                    e, half = u // 2, u % 2
                    for t in range(nd):
                        n = nd * u + t
                        pe.wait_ge(sem(f"gated{l}"), n + 1)
                        mm = pe.matmul(ps[:, 4 + half, :], w2[:, e, t, :], hg_ring[:, n % 8, :],
                                       start=False, stop=(e == E - 1 and t == nd - 1))
                        mm.then_inc(sem(f"down{l}"), 1)
                    return mm

                for u in range(2 * E):
                    up(u)
                    if u:
                        down(u - 1)
                down(2 * E - 1)

            def y_out(l):
                pe.wait_ge(sem(f"y_t{l}"), 1)
                for t in range(QT):
                    mm = pe.transpose(ps[:, t // 4, P * (t % 4):P * (t % 4) + P], y_t[:, P * t:P * t + P], ident_f[:, :])
                    if t % 4 == 3:
                        mm.then_inc(sem(f"turned_y{l}"), 1)

            pe.wait_ge(sem("ident"), 2)
            pe.wait_ge(sem("ones_set"), 1)
            pe.wait_ge(sem("att_w_in0"), ATT_IN)
            for c in range(NCH):
                keys(0, c)
            queries(0)
            attention(0, False)
            pe.wait_ge(sem("mask_tot"), 1)
            pe.wait_ge(sem("rank"), E + 3)
            pe.matmul(ps[0:1, 7, 0:1], m_tot[:, :], ones_f[:, :], start=True, stop=True).then_inc(sem("mask_all"), 1)
            attention_out(0)
            gating(0)
            experts(0)
            y_out(0)
            queries(1)
            pe.wait_ge(sem("flag_ready"), 1)
            with pe.If(pe.value_load(flag[0:1, 0:1], min_val=0, max_val=1) > 0):
                pe.wait_ge(sem("mask_turned"), NFULL // MCH + 1)
                attention(1, True)
            with pe.Else():
                attention(1, False)
            attention_out(1)
            gating(1)
            experts(1)
            y_out(1)


def kernel(x, ctx_1024, mask_Bx1xSxS2_bf1, g_xattn, g_ffn, **w):
    import concourse.bacc as bacc
    from concourse.bass_utils import run_bass_kernel_spmd

    nc = bacc.Bacc("TRN2", target_bir_lowering=False, num_devices=1)
    lay = np.ascontiguousarray
    arrays = {
        "x": lay(np.asarray(x).reshape(TQ, C)),
        "ctx_t": lay(np.asarray(ctx_1024).reshape(TK, C).T),
        "mask_t": lay(np.asarray(mask_Bx1xSxS2_bf1).reshape(TQ, TK).view(np.uint8).T),
        "g_xattn": lay(g_xattn), "g_ffn": lay(g_ffn),
        "gamma": lay(w["L0_ffn_gamma"]), "beta": lay(w["L0_ffn_beta"]), "br": lay(w["L1_ffn_br"]),
        "w_gate0": lay(np.asarray(w["L0_ffn_Wg"]).T), "w_gate1": lay(w["L1_ffn_Wr"]),
    }
    for l in range(2):
        for n in "qkvo":
            arrays[f"w{n}{l}"] = lay(np.asarray(w[f"L{l}_xattn_W{n}"]).T)
            bias = np.asarray(w[f"L{l}_xattn_b{n}"])
            arrays[f"b{n}{l}"] = lay(bias.reshape(C, 1) if n in "qk" else bias)
        arrays[f"w1_{l}"] = lay(w[f"L{l}_ffn_W1"])
        arrays[f"w2_{l}"] = lay(w[f"L{l}_ffn_W2"])
        arrays[f"b1_{l}"] = lay(np.asarray(w[f"L{l}_ffn_b1"]).reshape(E * FF // P, P).T)
        arrays[f"b2_{l}"] = lay(w[f"L{l}_ffn_b2"])
    arrays = {f"in_{n}": v for n, v in arrays.items()}
    args = {n[3:]: nc.dram_tensor(n, v.shape, mybir.dt.from_np(v.dtype), kind="ExternalInput").ap() for n, v in arrays.items()}
    out = nc.dram_tensor("out", [TQ, C], F32, kind="ExternalOutput").ap()
    block_kernel(nc, args, out)
    r = run_bass_kernel_spmd(nc, [arrays], core_ids=[0])
    return r.results[0]["out"].reshape(1, TQ, C)
```

```python
from contextlib import ExitStack

import concourse.bass as bass
import numpy as np
from concourse import mybir

F32 = mybir.dt.float32
BF16 = mybir.dt.bfloat16
F8 = mybir.dt.float8e5
U8 = mybir.dt.uint8
U16 = mybir.dt.uint16
I32 = mybir.dt.int32
ALU = mybir.AluOpType
ACT = mybir.ActivationFunctionType
AX = mybir.AxisListType

P = 128
C = 128
H = 16
HD = C // H
TQ = 1024
TK = 6404
QT = TQ // P
NFULL = TK // P
TAIL = TK - NFULL * P
NT = NFULL + 1
HALF = 512
E = 8
FF = 512
EPS = 1e-5
SCALE = float(HD) ** -0.5
MASKED = -1e20

PARTS = 3
KR = PARTS * HD
QKR = PARTS * KR
MROW = 96
ROWS_MAX = MROW
ROWS_EXP = MROW + PARTS
VW = HD + 1
QG = 4
QGW = TQ // QG
KST = 3
RING = 3
STEP = 2
NSTEP = -(-NT // STEP)
PSLOTS = 5
EXB = 3
V_CHUNKS = [(0, 12), (12, 24), (24, 36), (36, NT)]
AHEAD = 8
ENDING = [[("next", 0)], ["turn", ("next", 1)], [("next", 2), ("next", 3)], ["rows", ("next", 4)],
          [("next", 5)], [("next", 6), ("next", 7)]]
ENDING_UNITS = sum(ENDING, [])
AFTER_ROWS = len(ENDING_UNITS) - 1 - ENDING_UNITS.index("rows")
STEP_OUT = 1
STEPS_OF_3 = (4, 8, 12, 16)
MXU = NT + 3


def mx_steps(ahead):
    steps, t = [], AHEAD
    for s in range(NSTEP - len(ENDING)):
        n = 1 if s == 0 else 3 if s in STEPS_OF_3 else 2
        steps.append([("max", t + i) for i in range(n)] + ["out"] * (s == STEP_OUT))
        t += n
    assert t == NT
    return steps + [[u for u in step if ahead or isinstance(u, str)] for step in ENDING]


P_FIVES = NT - 4 * (-NT % 5)


def p_slot(t):
    return t % 5 if t < P_FIVES else (t - P_FIVES) % 4


def p_before(t):
    return max(u for u in range(-NT, t) if p_slot(u % NT) == p_slot(t))


assert MXU % 2 == 0 and AHEAD % 2 == 0 and 2 * NT % EXB == 0
assert P_FIVES % 5 == 0 and (NT - P_FIVES) % 4 == 0 and all(t - p_before(t) >= 4 for t in range(NT))


BF_ONES = float(np.array([0x3F803F80], np.uint32).view(np.float32)[0])
MCH = 5


def width(t):
    return P if t < NFULL else TAIL


def block_kernel(nc, a, out):
    with ExitStack() as ctx:
        def sb(name, shape, dt=F32):
            return ctx.enter_context(nc.sbuf_tensor(name, shape, dt))

        sems = {}

        def sem(name):
            if name not in sems:
                sems[name] = ctx.enter_context(nc.semaphore(name))
            return sems[name]

        k_parts = [nc.dram_tensor(f"k_parts{l}", [C, PARTS, TK], BF16, kind="Internal").ap() for l in range(2)]
        q_parts = [nc.dram_tensor(f"q_parts{l}", [C, PARTS, TQ], BF16, kind="Internal").ap() for l in range(2)]
        gate_rows = [nc.dram_tensor(f"gate_rows{l}", [E, TQ], F32, kind="Internal").ap() for l in range(2)]

        ps = ctx.enter_context(nc.psum_tensor("ps", [P, 8, HALF], F32))

        def flat3(t):
            return t[:, :, :].rearrange("p a b -> p (a b)")

        ctx_t = sb("ctx_t", [P, TK])
        w1_1 = ctx_t[:, 0:E * FF].rearrange("p (e f) -> p e f", e=E)
        w2_1 = ctx_t[:, E * FF:E * FF + E * 2 * C].rearrange("p (e t d) -> p e t d", e=E, t=2)
        k_ring = sb("k_ring", [P, RING * TK], BF16)
        q_ring = sb("q_ring", [P, RING * TQ], BF16)
        gate_bc = k_ring[:, 0:E * TQ * 2].bitcast(F32).rearrange("p (e q) -> p e q", e=E)
        v_all = sb("v_all", [P, NT, H, VW])
        v_head = sb("v_head", [P, NT, VW])
        probs = sb("probs", [P, PSLOTS + 1, TQ])
        m_join = probs[:, PSLOTS, :]
        mask_stage = [flat3(probs)[:, n * MCH * TQ // 4:(n + 1) * MCH * TQ // 4].bitcast(U8) for n in range(2)]
        mask_junk = flat3(probs)[:, 3 * TQ:3 * TQ + MCH * TQ // 4].bitcast(BF16)
        h_ring = probs[:, 0:2, :].rearrange("p a (b c) -> p (a b) c", b=2)
        hg_ring = probs[:, 2:6, :].rearrange("p a (b c) -> p (a b) c", b=2)
        big = sb("big", [P, NT * TQ // 4])
        w1_0 = big[:, 0:E * FF].rearrange("p (e f) -> p e f", e=E)
        w2_0 = big[:, E * FF:2 * E * FF].rearrange("p (e t d) -> p e t d", e=E, t=4)
        mask_n = big[:, :].bitcast(F8).rearrange("p (t q) -> p t q", t=NT)
        spare = big[:, 2 * E * FF:]
        k_f = spare[:, 0:2 * HALF].rearrange("p (a w) -> p a w", a=2)
        k_rest = spare[:, 2 * HALF:4 * HALF].rearrange("p (a w) -> p a w", a=2)
        k_st = spare[:, 4 * HALF:4 * HALF + KST * PARTS * HALF // 2].bitcast(BF16).rearrange("p (a b w) -> p a b w", a=KST, b=PARTS)
        gate_t = spare[0:E, 7 * HALF:7 * HALF + TQ]
        q_f = probs[:, 0, :].rearrange("p (a w) -> p a w", a=2)
        q_rest = probs[:, 1, :].rearrange("p (a w) -> p a w", a=2)
        q_st = flat3(probs)[:, 2 * TQ:2 * TQ + PARTS * HALF].bitcast(BF16).rearrange("p (a b w) -> p a b w", a=2, b=PARTS)
        m_run = sb("m_run", [P, 2, TQ])
        x_t = m_run[:, 0, :]
        y_t = m_run[:, 1, :]
        x_n = y_t.rearrange("p (t c) -> p t c", c=C)
        x_sb = sb("x_sb", [P, QT, C])
        o_all = sb("o_all", [P, QT, (H + 1) * HD])
        x_ln = flat3(o_all)[:, 0:QT * C].rearrange("p (t c) -> p t c", c=C)
        o_raw = sb("o_raw", [P, QGW])
        m_neg = sb("m_neg", [P, 2, QT])
        m_pad = sb("m_pad", [P, QT, P], BF16)
        r_den = sb("r_den", [P, QT])
        w_att = sb("w_att", [P, 2, 4, C])
        b_col = sb("b_col", [P, 2, 2])
        b_row = sb("b_row", [P, 2, 2, C])
        gb_row = sb("gb_row", [P, 2, C])
        w_gate = sb("w_gate", [P, 2, E])
        br_row = sb("br_row", [P, E])
        b1_col = sb("b1_col", [P, 2, E * 4])
        b2_sb = sb("b2_sb", [E, 2, C])
        g_raw = sb("g_raw", [P, 4])
        g_tanh = sb("g_tanh", [P, 4])
        ident_f = sb("ident_f", [P, P])
        ident_b = sb("ident_b", [P, P], BF16)
        neg_i = sb("neg_i", [P, P], BF16)
        ones_f = sb("ones_f", [P, 1])
        ones_b = sb("ones_b", [P, QGW], BF16)
        rank = sb("rank", [P, E])
        st = sb("st", [P, QT, 6])
        mv = sb("mv", [P, QT, 2])
        var_e = sb("var_e", [P, QT])
        std = sb("std", [P, QT])
        r_std = sb("r_std", [P, QT])
        ga = sb("ga", [P, 6, QT, E])
        gs = sb("gs", [P, 6, QT])
        m_sum = sb("m_sum", [P, NFULL // MCH + 1])
        m_tot = sb("m_tot", [P, 1])
        flag_f = sb("flag_f", [1, 1])
        flag = sb("flag", [1, 1], I32)

        def exp_banks(l, h):
            return [4, 5, 6] + [2, 3] * (l == 1 and isinstance(h, int) and h == H - 1)

        def mx(slot):
            return ps[:, 2 * slot:2 * slot + 2, :]

        def flat(ap):
            return ap.rearrange("p a b -> p (a b)")

        NCH = -(-TK // HALF)
        chunk_w = [min(HALF, TK - HALF * c) for c in range(NCH)]
        CTX_CHUNKS = [(0, 2 * HALF), (2 * HALF, 6 * HALF), (6 * HALF, TK)]
        ATT_IN, SMALL_IN = 8 * 16, 16 * 9
        FIRST = NT + len(ENDING_UNITS)
        HEAD_IN = 2 * PARTS * 16
        FIRST_IN = [[HEAD_IN * (h + 1) for h in range(RING)],
                    [HEAD_IN // 2 * (RING + h + 1) for h in range(RING)]]
        LOOP = H - 2
        LAST2 = FIRST + MXU * LOOP
        LAST = LAST2 + MXU - AHEAD
        MX_OUT = sum(len(u) for u in mx_steps(True)[:STEP_OUT + 1])


        def wait_apart(eng, name, s, value, apart=True):
            eng.wait_ge(s, value)
            if apart and not isinstance(value, int):
                eng.sem_inc(sem(f"{name}_apart"), 1)

        def attention_weights(eng, l):
            for w in "kqvo":
                eng.dma_start(w_att[:, l, "qkvo".index(w), :], a[f"w{w}{l}"]).then_inc(sem(f"att_w_in{l}"), 16)
            for n, w in enumerate("qk"):
                eng.dma_start(b_col[:, l, n:n + 1], a[f"b{w}{l}"]).then_inc(sem(f"att_w_in{l}"), 16)
            for n, w in enumerate("vo"):
                eng.dma_start(b_row[:, l, n, :], a[f"b{w}{l}"].partition_broadcast(P)).then_inc(sem(f"att_w_in{l}"), 16)

        block = ctx.enter_context(nc.Block())

        @block.sync
        def _(sp):
            def setup():
                for c0, c1 in CTX_CHUNKS:
                    sp.dma_start(ctx_t[:, c0:c1], a["ctx_t"][:, c0:c1]).then_inc(sem(f"ctx_in{c0}"), 16)
                attention_weights(sp, 1)
                for l in range(2):
                    sp.dma_start(w_gate[:, l, :], a[f"w_gate{l}"]).then_inc(sem("small_in"), 16)
                    sp.dma_start(b1_col[:, l, :], a[f"b1_{l}"]).then_inc(sem("small_in"), 16)
                    sp.dma_start(b2_sb[:, l, :], a[f"b2_{l}"]).then_inc(sem("small_in"), 16)
                for n, w in enumerate(("gamma", "beta")):
                    sp.dma_start(gb_row[:, n, :], a[w].partition_broadcast(P)).then_inc(sem("small_in"), 16)
                sp.dma_start(br_row[:, :], a["br"].partition_broadcast(P)).then_inc(sem("small_in"), 16)
                sp.dma_start(w1_0, a["w1_0"].rearrange("e d f -> d e f")).then_inc(sem("experts_in0"), 16)
                sp.dma_start(w2_0.rearrange("p e t d -> p (e t) d"),
                             a["w2_0"].rearrange("e (t f) d -> f (e t) d", f=P)).then_inc(sem("experts_in0"), 16)

            def store_k(l):
                for c in range(NCH):
                    sp.wait_ge(sem(f"k_split{l}"), c + 1)
                    sp.dma_start(k_parts[l][:, :, HALF * c:HALF * c + chunk_w[c]],
                                 k_st[:, c % KST, :, 0:chunk_w[c]]).then_inc(sem(f"k_stored{l}_{c % KST}"), 16)

            def store_q(l):
                for half in range(2):
                    sp.wait_ge(sem(f"q_split{l}"), half + 1)
                    sp.dma_start(q_parts[l][:, :, HALF * half:HALF * half + HALF], q_st[:, half, :, :]).then_inc(sem(f"q_stored{l}"), 16)

            def check_mask():
                for c in range(NFULL // MCH):
                    if c > 1:
                        sp.wait_ge(sem("mask_summed"), c - 1)
                    sp.dma_start(mask_stage[c % 2].rearrange("p (t q) -> p t q", q=TQ),
                                 a["mask_t"][c * MCH * P:(c + 1) * MCH * P, :].rearrange("(t p) q -> p t q", p=P)
                                 ).then_inc(sem(f"mask_in{c % 2}"), 16)
                sp.wait_ge(sem("mask_summed"), NFULL // MCH - 1)
                sp.dma_start(mask_stage[0][0:TAIL, 0:TQ], a["mask_t"][NFULL * P:TK, :]).then_inc(sem("mask_in0"), 16)

            def build_mask():
                sp.wait_ge(sem("flag_ready"), 1)
                sp.wait_ge(sem("ffn_done0"), 1)
                with sp.If(sp.value_load(flag[0:1, 0:1], min_val=0, max_val=1) > 0):
                    for c in range(NFULL // MCH):
                        if c:
                            sp.wait_ge(sem("mask_turned"), c)
                        sp.dma_start(mask_stage[0].rearrange("p (t q) -> p t q", q=TQ),
                                     a["mask_t"][c * MCH * P:(c + 1) * MCH * P, :].rearrange("(t p) q -> p t q", p=P)
                                     ).then_inc(sem("mask_again"), 16)
                    sp.wait_ge(sem("mask_turned"), NFULL // MCH)
                    sp.dma_start(mask_stage[0][0:TAIL, 0:TQ], a["mask_t"][NFULL * P:TK, :]).then_inc(sem("mask_again"), 16)
                with sp.Else():
                    sp.nop()

            def place(h, w):
                return h % RING * w if isinstance(h, int) else sp.snap((h % RING) * w)

            def load_keys(l, h):
                koff = place(h, TK)
                for b in range(PARTS):
                    sp.dma_start(k_ring[b * KR:(b + 1) * KR, bass.ds(koff, TK)],
                                 k_parts[l][bass.ds(h * HD, HD)].rearrange("d a w -> a d w")
                                 ).then_inc(sem(f"head_in{l}"), 16)

            def load_queries(l, h):
                qoff = place(h, TQ)
                for b in range(PARTS):
                    part = q_parts[l][bass.ds(h * HD, HD), b:b + 1, :].rearrange("d o w -> o d w")
                    sp.dma_start(q_ring[b * KR:(b + 1) * KR, bass.ds(qoff, TQ)], part.broadcast_to([PARTS, HD, TQ])
                                 ).then_inc(sem(f"head_in{l}"), 16)

            def ready(l, what):
                if what == "q":
                    sp.wait_ge(sem(f"q_stored{l}"), 16 * 2)
                else:
                    for n in range(KST):
                        sp.wait_ge(sem(f"k_stored{l}_{n}"), 16 * len(range(n, NCH, KST)))

            def load_first(l):
                sp.wait_ge(sem("ring_set"), l + 2)
                sp.wait_ge(sem("ring_ones"), l + 1)
                if l:
                    ready(l, "k")
                    for h in range(RING):
                        load_keys(l, h)
                    store_q(l)
                ready(l, "q")
                if l:
                    sp.wait_ge(sem("head_in1"), FIRST_IN[l][0] - HEAD_IN // 2)
                for h in range(RING):
                    load_queries(l, h)
                    if l == 0:
                        ready(l, "k")
                        load_keys(l, h)
                    sp.wait_ge(sem(f"head_in{l}"), FIRST_IN[l][h])

            def load_heads(l):
                with sp.Fori(RING, H) as h:
                    wait_apart(sp, "sp", sem(f"scored{l}"), h * (2 * NT) - (RING - 1) * 2 * NT)
                    load_keys(l, h)
                    load_queries(l, h)
                    wait_apart(sp, "sp", sem(f"head_in{l}"), HEAD_IN * h + HEAD_IN)

            def spread_gates(l):
                sp.wait_ge(sem(f"gate_t{l}"), 1)
                sp.dma_start(gate_rows[l], gate_t[:, :]).then_inc(sem(f"gate_out{l}"), 16)
                sp.wait_ge(sem(f"gate_out{l}"), 16)
                for e in range(E):
                    sp.dma_start(gate_bc[:, e, :], gate_rows[l][e:e + 1, :].rearrange("e q -> (e q)").partition_broadcast(P)
                                 ).then_inc(sem(f"gate_bc{l}_{e}"), 16)

            sp.dma_start(x_sb[:, :, :], a["x"].rearrange("(t p) c -> p t c", p=P)).then_inc(sem("x_in"), 16)
            setup()
            store_q(0)
            store_k(0)
            load_first(0)
            check_mask()
            load_heads(0)
            store_k(1)
            sp.wait_ge(sem("v_proj1"), NCH)
            sp.wait_ge(sem("k_proj1"), NCH)
            sp.dma_start(w1_1, a["w1_1"].rearrange("e d f -> d e f")).then_inc(sem("experts_in1"), 16)
            sp.dma_start(w2_1.rearrange("p e t d -> p (e t) d"),
                         a["w2_1"].rearrange("e (t f) d -> f (e t) d", f=P)).then_inc(sem("experts_in1"), 16)
            spread_gates(0)
            load_first(1)
            build_mask()
            load_heads(1)
            spread_gates(1)
            sp.wait_ge(sem("x_final"), 1)
            sp.dma_start(out.rearrange("(t p) c -> p t c", p=P), x_sb[:, :, :]).then_inc(sem("out_stored"), 16)
            sp.wait_ge(sem("out_stored"), 16)

        @block.gpsimd
        def _(pool):
            chain = [0]

            def link(ins):
                chain[0] += 1
                ins.then_inc(sem("pool_chain"), 1)
                pool.wait_ge(sem("pool_chain"), chain[0])

            def set_ring(l):
                if l:
                    pool.wait_ge(sem("v_head0"), H * len(V_CHUNKS))
                    pool.wait_ge(sem("gated0"), 2 * E * 4)
                else:
                    pool.wait_ge(sem("ones_set"), 1)
                nc.gpsimd.memset(k_ring[MROW:P, :].bitcast(F32), BF_ONES).then_inc(sem("ring_ones"), 1)
                pool.wait_ge(sem("ring_ones"), l + 1)
                if l == 0:
                    nc.gpsimd.memset(k_ring[2 * 32:MROW, :].bitcast(F32), 0.0).then_inc(sem("ring_set"), 1)
                    pool.wait_ge(sem("ring_set"), 2)

            def constants():
                link(nc.gpsimd.memset(ident_f[:, :], 0.0))
                nc.gpsimd.affine_select(out=ident_f[:, :], in_=ident_f[:, :], compare_op=ALU.not_equal, fill=1.0,
                                        base=0, pattern=[[-1, P]], channel_multiplier=1).then_inc(sem("ident"), 1)
                pool.wait_ge(sem("ident"), 1)
                nc.gpsimd.tensor_copy(ident_b[:, :], ident_f[:, :]).then_inc(sem("ident"), 1)
                nc.gpsimd.memset(ones_b[:, :], 1.0).then_inc(sem("ones_set"), 1)
                set_ring(0)
                for e in range(E):
                    nc.gpsimd.memset(rank[:, e:e + 1], float(E - e)).then_inc(sem("rank"), 1)
                nc.gpsimd.memset(ones_f[:, :], 1.0).then_inc(sem("rank"), 1)
                nc.gpsimd.memset(m_pad[:, :, :], 0.0).then_inc(sem("rank"), 1)
                nc.gpsimd.tensor_scalar(neg_i[:, :], ident_f[:, :], MASKED, 0.0, ALU.mult, ALU.add).then_inc(sem("rank"), 1)
                pool.wait_ge(sem("rank"), E + 3)

            def v_chunk(l, h, n):
                t0, t1 = V_CHUNKS[n]
                nc.gpsimd.tensor_copy(v_head[:, t0:t1, :], v_all[:, t0:t1, bass.ds(h, 1), :].rearrange("p t o d -> p t (o d)")
                                      ).then_inc(sem(f"v_head{l}"), 1)

            def v_heads(l):
                pool.wait_ge(sem(f"v_set{l}"), NCH + 1)
                if l == 0:
                    pool.wait_ge(sem("v_init"), 2)
                for n in range(len(V_CHUNKS)):
                    v_chunk(l, 0, n)
                with pool.Fori(1, H) as h:
                    for n, (_, t1) in enumerate(V_CHUNKS):
                        pool.wait_ge(sem(f"pv_done{l}"), h * NT + t1)
                        v_chunk(l, h, n)

            constants()
            v_heads(0)
            set_ring(1)
            v_heads(1)

        @block.scalar
        def _(act):
            A = nc.scalar.activation

            def project_k():
                for c in range(NCH):
                    w = chunk_w[c]
                    act.wait_ge(sem("k_proj0"), c + 1)
                    if c >= 2:
                        act.wait_ge(sem("k_split0"), c - 1)
                    if c >= KST:
                        act.wait_ge(sem(f"k_stored0_{c % KST}"), 16 * (c // KST))
                    A(k_f[:, c % 2, 0:w], ps[:, c % 2, 0:w], ACT.Identity, bias=b_col[:, 0, 1:2]).then_inc(sem("k_evac0"), 1)
                    A(k_st[:, c % KST, 0, 0:w], ps[:, c % 2, 0:w], ACT.Identity, bias=b_col[:, 0, 1:2]).then_inc(sem("k_evac0"), 1)

            def set_v(c):
                n = min(4, NFULL - 4 * c)
                act.wait_ge(sem("v_proj0"), c + 1)
                bank = ps[:, 4 + c % 4, :].rearrange("p (t h d) -> p t h d", t=4, h=H)
                A(v_all[:, 4 * c:4 * c + n, :, 0:HD], bank[:, 0:n], ACT.Identity).then_inc(sem("v_set0"), 1)
                if c == NCH - 1:
                    act.wait_ge(sem("v_init"), 2)
                    A(v_all[0:TAIL, NFULL:NT, :, 0:HD], bank[0:TAIL, n:n + 1], ACT.Identity).then_inc(sem("v_set0"), 1)

            def std_of(tag):
                act.wait_ge(sem(f"var_{tag}"), 1)
                A(std[:, :], var_e[:, :], ACT.Sqrt).then_inc(sem(f"std_{tag}"), 1)

            def turned(tag, bank, dst):
                for half in range(2):
                    act.wait_ge(sem(f"turned_{tag}"), half + 1)
                    A(dst[:, HALF * half:HALF * half + HALF], ps[:, bank + half, :], ACT.Identity).then_inc(sem(f"copied_{tag}"), 1)

            def project_q(l):
                turned(f"q{l}", 4, x_t)
                for half in range(2):
                    act.wait_ge(sem(f"q_proj{l}"), half + 1)
                    A(q_f[:, half, :], ps[:, 6 + half, :], ACT.Identity, bias=b_col[:, l, 0:1]).then_inc(sem(f"q_evac{l}"), 1)
                    A(q_st[:, half, 0, :], ps[:, 6 + half, :], ACT.Identity, bias=b_col[:, l, 0:1]).then_inc(sem(f"q_evac{l}"), 1)

            def sum_mask(c):
                act.wait_ge(sem(f"mask_in{c % 2}"), 16 * (c // 2 + 1))
                rows, n = (P, MCH * TQ // 2) if c < NFULL // MCH else (TAIL, TQ // 2)
                if c:
                    act.wait_ge(sem("mask_summed"), c)
                A(mask_junk[0:rows, 0:n], mask_stage[c % 2][0:rows, 0:2 * n].bitcast(U16), ACT.Copy,
                  accum_out=m_sum[0:rows, c:c + 1]).then_inc(sem("mask_summed"), 1)

            def evacuate(l, h, out_unit):
                act.wait_ge(sem(f"pv_done{l}"), h * NT + NT)
                act.wait_ge(sem(f"mx_filled{l}"), out_unit)
                A(o_raw[:, :], ps[:, 7, 0:QGW], ACT.Identity).then_inc(sem(f"o_raw{l}"), 1)

            def exp_head(l, h, out_unit):
                for t in range(NT):
                    k = width(t)
                    act.wait_ge(sem(f"pv_done{l}"), h * NT + (NT + p_before(t) + 1))
                    for half in range(2):
                        u = 2 * t + half
                        act.wait_ge(sem(f"scored{l}"), h * (2 * NT) + (u + 1))
                        bank = exp_banks(l, h)[u % len(exp_banks(l, h))]
                        A(probs[0:k, p_slot(t), HALF * half:HALF * half + HALF], ps[0:k, bank, :], ACT.Exp,
                          scale=SCALE).then_inc(sem(f"exp_done{l}"), 1)
                    if t == STEP - 1:
                        evacuate(l, h, out_unit)

            def exp_all(l):
                act.nop().then_inc(sem(f"exp_done{l}"), EXB)
                with act.Fori(0, LOOP) as h:
                    exp_head(l, h, h * MXU + (FIRST + MX_OUT - MXU))
                exp_head(l, H - 2, LAST2 + MX_OUT - MXU)
                exp_head(l, H - 1, LAST2 + MX_OUT)
                evacuate(l, H, LAST + 1)

            def gates(l):
                act.wait_ge(sem(f"gate_in{l}"), 1)
                A(ga[:, 1, :, :], ga[:, 0, :, :], ACT.Exp).then_inc(sem(f"gate_exp{l}"), 1)

            def gates_turned(l):
                act.wait_ge(sem(f"gate_turned{l}"), 1)
                if l == 0:
                    for n in range(KST):
                        act.wait_ge(sem(f"k_stored1_{n}"), 16 * len(range(n, NCH, KST)))
                A(gate_t[:, :], flat(ps[0:E, 6:8, :]), ACT.Identity).then_inc(sem(f"gate_t{l}"), 1)

            def experts0():
                for u in range(E * 2 * 4):
                    e, t = u // 8, u % 4
                    if u == 4:
                        gates_turned(0)
                    act.wait_ge(sem("hidden0"), u + 1)
                    if u >= 4:
                        act.wait_ge(sem("gated0"), u - 3)
                    A(h_ring[:, u % 4, :], ps[:, u % 4, :], ACT.Gelu_apprx_tanh,
                      bias=b1_col[:, 0, e * 4 + t:e * 4 + t + 1]).then_inc(sem("act_done0"), 1)

            def experts1():
                for u in range(E * 2):
                    e = u // 2
                    if u == 1:
                        gates_turned(1)
                    act.wait_ge(sem("hidden1"), 4 * u + 2)
                    for t in range(2):
                        if u >= 2:
                            act.wait_ge(sem("gated1"), 2 * (u - 2) + t + 1)
                        A(h_ring[:, 2 * (u % 2) + t, :], ps[:, t, :], ACT.Silu,
                          bias=b1_col[:, 1, e * 4 + t:e * 4 + t + 1]).then_inc(sem("act_done1"), 1)

            def y_out(l):
                for half in range(2):
                    act.wait_ge(sem(f"y_sum{l}"), half + 1)
                    A(y_t[:, HALF * half:HALF * half + HALF], ps[:, 4 + half, :], ACT.Identity).then_inc(sem(f"y_t{l}"), 1)

            attention_weights(act, 0)
            act.dma_start(g_raw[:, 0:2], a["g_xattn"].partition_broadcast(P)).then_inc(sem("g_in"), 16)
            act.dma_start(g_raw[:, 2:4], a["g_ffn"].partition_broadcast(P)).then_inc(sem("g_in"), 16)
            std_of("q0")
            act.wait_ge(sem("g_in"), 32)
            A(g_tanh[:, :], g_raw[:, :], ACT.Tanh).then_inc(sem("g_tanh"), 1)
            act.wait_ge(sem("att_w_in0"), ATT_IN)
            project_q(0)
            project_k()
            for c in range(NCH):
                set_v(c)
                if c < NFULL // MCH + 1:
                    sum_mask(c)
            act.wait_ge(sem("mask_summed"), NFULL // MCH + 1)
            exp_all(0)
            turned("o0", 0, x_t)
            std_of("f0")
            std_of("g0")
            turned("f0", 0, x_t)
            gates(0)
            experts0()
            y_out(0)
            std_of("q1")
            project_q(1)
            exp_all(1)
            turned("o1", 0, x_t)
            std_of("f1")
            turned("f1", 0, x_t)
            gates(1)
            experts1()
            y_out(1)

        @block.vector
        def _(dve):
            V = nc.vector
            chain = [0]

            def link(ins):
                chain[0] += 1
                ins.then_inc(sem("dve_chain"), 1)
                dve.wait_ge(sem("dve_chain"), chain[0])

            def note(ins):
                chain[0] += 1
                ins.then_inc(sem("dve_chain"), 1)

            def settle():
                dve.wait_ge(sem("dve_chain"), chain[0])

            def layer_norm(tag, src, dst, done=None):
                for t in range(QT):
                    note(V.bn_stats(st[:, t, :], src[:, t, :]))
                settle()
                for t in range(QT):
                    note(V.bn_aggr(mv[:, t, :], st[:, t, :]))
                settle()
                V.tensor_scalar(var_e[:, :], mv[:, :, 1], EPS, None, ALU.add).then_inc(sem(f"var_{tag}"), 1)
                dve.wait_ge(sem(f"std_{tag}"), 1)
                link(V.reciprocal(r_std[:, :], std[:, :]))
                for t in range(QT):
                    ins = V.tensor_scalar(dst[:, t, :], src[:, t, :], mv[:, t, 0:1], r_std[:, t:t + 1],
                                          ALU.subtract, ALU.mult)
                    ins.then_inc(sem(done), 1) if done else note(ins)
                settle()

            def split(f, parts, rest, w):
                link(V.tensor_tensor(rest[:, 0:w], f[:, 0:w], parts[:, 0, 0:w], ALU.subtract))
                link(V.tensor_copy(parts[:, 1, 0:w], rest[:, 0:w]))
                return V.tensor_tensor(parts[:, 2, 0:w], rest[:, 0:w], parts[:, 1, 0:w], ALU.subtract)

            def split_keys():
                for c in range(NCH):
                    dve.wait_ge(sem("k_evac0"), 2 * (c + 1))
                    split(k_f[:, c % 2, :], k_st[:, c % KST, :, :], k_rest[:, c % 2, :], chunk_w[c]).then_inc(sem("k_split0"), 1)

            def next_keys_values():
                dve.wait_ge(sem("v_head0"), H * len(V_CHUNKS))
                dve.wait_ge(sem("att_w_in1"), ATT_IN)
                for c in range(NCH):
                    w = chunk_w[c]
                    dve.wait_ge(sem("k_proj1"), c + 1)
                    if c >= KST:
                        dve.wait_ge(sem(f"k_stored1_{c % KST}"), 16 * (c // KST))
                    for dst in (k_f[:, c % 2, 0:w], k_st[:, c % KST, 0, 0:w]):
                        ins = V.tensor_scalar(dst, ps[:, c % 2, 0:w], b_col[:, 1, 1:2], None, ALU.add)
                        ins.then_inc(sem("k_evac1"), 1)
                    dve.wait_ge(sem("k_evac1"), 2 * (c + 1))
                    split(k_f[:, c % 2, :], k_st[:, c % KST, :, :], k_rest[:, c % 2, :], w).then_inc(sem("k_split1"), 1)
                    n = min(4, NFULL - 4 * c)
                    dve.wait_ge(sem("v_proj1"), c + 1)
                    bank = ps[:, 2 + c % 2, :].rearrange("p (t h d) -> p t h d", t=4, h=H)
                    V.tensor_copy(v_all[:, 4 * c:4 * c + n, :, 0:HD], bank[:, 0:n]).then_inc(sem("v_set1"), 1)
                    if c == NCH - 1:
                        V.tensor_copy(v_all[0:TAIL, NFULL:NT, :, 0:HD], bank[0:TAIL, n:n + 1]).then_inc(sem("v_set1"), 1)

            def set_ring():
                dve.wait_ge(sem("gated0"), 2 * E * 4)
                V.memset(k_ring[2 * 32:MROW, :].bitcast(F32), 0.0).then_inc(sem("ring_set"), 1)

            def queries(l):
                for half in range(2):
                    dve.wait_ge(sem(f"q_evac{l}"), 2 * (half + 1))
                    split(q_f[:, half, :], q_st[:, half, :, :], q_rest[:, half, :], HALF).then_inc(sem(f"q_split{l}"), 1)

            def max_tile(l, h, unit, t, slot):
                k = width(t)
                dve.wait_ge(sem(f"mx_filled{l}"), unit + 1)
                if t >= 2:
                    dve.wait_ge(sem(f"mx_done{l}"), unit - 1)
                    V.tensor_tensor(m_run[0:k, t % 2, :], flat(mx(slot)[0:k]), m_run[0:k, t % 2, :], ALU.max
                                    ).then_inc(sem(f"mx_done{l}"), 1)
                else:
                    if not (isinstance(h, int) and h == 0):
                        dve.wait_ge(sem(f"m_joined{l}"), h)
                    V.tensor_copy(m_run[:, t, :], flat(mx(slot))).then_inc(sem(f"mx_done{l}"), 1)

            def join(l, unit):
                dve.wait_ge(sem(f"mx_done{l}"), unit + 1)
                V.tensor_tensor(m_join, m_run[:, 0, :], m_run[:, 1, :], ALU.max).then_inc(sem(f"m_joined{l}"), 1)

            def reduce_max(l, h, unit, slot):
                dve.wait_ge(sem(f"mx_filled{l}"), unit + 1)
                V.tensor_reduce(m_neg[:, 0, :], flat(mx(slot)).rearrange("p (t k) -> p t k", k=P), AX.X, ALU.max,
                                negate=True).then_inc(sem(f"mx_done{l}"), 1)
                dve.wait_ge(sem(f"mx_done{l}"), unit + 1)
                V.tensor_copy(m_pad[:, :, MROW], m_neg[:, 0, :]).then_inc(sem(f"m_split{l}"), 1)
                dve.wait_ge(sem(f"m_split{l}"), h * 4 + 1)
                V.tensor_tensor(m_neg[:, 1, :], m_neg[:, 0, :], m_pad[:, :, MROW], ALU.subtract).then_inc(sem(f"m_split{l}"), 1)
                dve.wait_ge(sem(f"m_split{l}"), h * 4 + 2)
                V.tensor_copy(m_pad[:, :, MROW + 1], m_neg[:, 1, :]).then_inc(sem(f"m_split{l}"), 1)
                dve.wait_ge(sem(f"m_split{l}"), h * 4 + 3)
                V.tensor_tensor(m_pad[:, :, MROW + 2], m_neg[:, 1, :], m_pad[:, :, MROW + 1], ALU.subtract
                                ).then_inc(sem(f"m_split{l}"), 1)

            def set_rows(l, h, unit, slot):
                dve.wait_ge(sem(f"mx_filled{l}"), unit + 1)
                V.tensor_copy(q_ring[MROW:MROW + PARTS, bass.ds((h % RING) * TQ, TQ)],
                              ps[MROW:MROW + PARTS, 2 * slot, :].bitcast(BF16)).then_inc(sem(f"mx_done{l}"), 1)

            def o_norm(l, h, base, slot):
                o = mx(slot)[:, 0, 0:2 * P].rearrange("p (c g d) -> p c g d", c=2, g=QG)
                dve.wait_ge(sem(f"mx_filled{l}"), base + 1)
                V.reciprocal(r_den[:, :].rearrange("p (c g) -> p c g", c=2), o[:, :, :, HD]).then_inc(sem(f"r_den{l}"), 1)
                dve.wait_ge(sem(f"r_den{l}"), h + 1)
                V.tensor_tensor(o_all[:, :, bass.ds(h * HD, HD)].rearrange("p (g c) d -> p c g d", c=2), o[:, :, :, 0:HD],
                                r_den[:, :].rearrange("p (c g o) -> p c g o", c=2, o=1).broadcast_to([P, 2, QG, HD]),
                                ALU.mult).then_inc(sem(f"mx_done{l}"), 1)

            def one_unit(l, h, kind, unit, slot):
                if kind == "out":
                    o_norm(l, h, unit, slot)
                elif kind == "turn":
                    reduce_max(l, h + 1, unit, slot)
                elif kind == "rows":
                    set_rows(l, h + 1, unit, slot)
                else:
                    what, t = kind
                    max_tile(l, h + (1 if what == "max" else 2), unit, t, slot)
                    if t == NT - 1:
                        join(l, unit)

            def maxima(l):
                dve.wait_ge(sem("rank"), E + 3)
                for unit, kind in enumerate([("max", t) for t in range(NT)] + ENDING_UNITS):
                    one_unit(l, -1, kind, unit, (unit + FIRST) % 2)
                with dve.Fori(0, LOOP) as h:
                    base = dve.snap(h * MXU)
                    for j, kind in enumerate(k for step in mx_steps(True) for k in step):
                        one_unit(l, h, kind, base + (FIRST + j), j % 2)
                for j, kind in enumerate(k for step in mx_steps(False) for k in step):
                    one_unit(l, H - 2, kind, LAST2 + j, j % 2)
                o_norm(l, H - 1, LAST, 0)
                dve.wait_ge(sem(f"mx_done{l}"), LAST + 1)
                if l == 0:
                    next_keys_values()
                    total_mask()
                def add_bias(c0, c1):
                    V.tensor_tensor(o_all[:, :, HD + c0:HD + c1], o_all[:, :, HD + c0:HD + c1],
                                    b_row[:, l, 0:1, c0:c1].broadcast_to([P, QT, c1 - c0]), ALU.add
                                    ).then_inc(sem(f"o_biased{l}"), 1)

                add_bias(0, C - HD)
                o_norm(l, H, LAST + 1, 1)
                dve.wait_ge(sem(f"mx_done{l}"), LAST + 2)
                add_bias(C - HD, C)

            def attention_out(l):
                dve.wait_ge(sem("g_tanh"), 1)
                dve.wait_ge(sem(f"o_proj{l}"), 2)
                bias = b_row[:, l, 1:2, :].broadcast_to([P, QT, C])
                V.tensor_tensor(x_ln[:, :, :], flat(ps[:, 2:4, :]).rearrange("p (t c) -> p t c", c=C), bias, ALU.add
                                ).then_inc(sem(f"att_added{l}"), 1)
                dve.wait_ge(sem(f"att_added{l}"), 1)
                link(V.scalar_tensor_tensor(out=flat(x_sb), in0=flat(x_ln), scalar=g_tanh[:, l:l + 1], in1=flat(x_sb),
                                            op0=ALU.mult, op1=ALU.add))

            def total_mask():
                n = NFULL // MCH
                dve.wait_ge(sem("mask_summed"), n + 1)
                link(V.tensor_scalar(m_sum[:, 0:n], m_sum[:, 0:n], -257.0 * MCH * TQ / 2, None, ALU.add))
                link(V.tensor_scalar(m_sum[0:TAIL, n:n + 1], m_sum[0:TAIL, n:n + 1], -257.0 * TQ / 2, None, ALU.add))
                link(V.tensor_reduce(m_tot[:, :], m_sum[:, 0:n], AX.X, ALU.add))
                V.tensor_tensor(m_tot[0:TAIL, :], m_tot[0:TAIL, :], m_sum[0:TAIL, n:n + 1], ALU.add).then_inc(sem("mask_tot"), 1)

            def set_flag():
                dve.wait_ge(sem("mask_all"), 1)
                link(V.tensor_scalar(flag_f[:, :], ps[0:1, 7, 0:1], -0.5, None, ALU.is_lt))
                V.tensor_copy(flag[:, :], flag_f[:, :]).then_inc(sem("flag_ready"), 1)

            def top_two(l):
                logit, prob, tmp, one1, gate, one2 = (ga[:, n, :, :] for n in range(6))

                def spread(n):
                    return gs[:, n, :].rearrange("p (t o) -> p t o", o=1).broadcast_to([P, QT, E])

                rank_b = rank[:, :].rearrange("p (o e) -> p o e", o=1).broadcast_to([P, QT, E])
                raw = ps[:, 7, 0:QT * E].rearrange("p (t e) -> p t e", e=E)
                dve.wait_ge(sem(f"logits{l}"), 1)
                dve.wait_ge(sem("rank"), E + 3)
                if l:
                    link(V.tensor_tensor(tmp, raw, br_row[:, :].rearrange("p (o e) -> p o e", o=1).broadcast_to([P, QT, E]), ALU.add))
                else:
                    link(V.tensor_copy(tmp, raw))
                link(V.tensor_reduce(gs[:, 0, :], tmp, AX.X, ALU.max))
                V.tensor_tensor(logit, tmp, spread(0), ALU.subtract).then_inc(sem(f"gate_in{l}"), 1)
                dve.wait_ge(sem(f"gate_exp{l}"), 1)
                pick, low = tmp, -3e38
                if l == 0:
                    link(V.tensor_reduce(gs[:, 1, :], prob, AX.X, ALU.add))
                    link(V.reciprocal(gs[:, 2, :], gs[:, 1, :]))
                    link(V.tensor_tensor(prob, prob, spread(2), ALU.mult))
                    pick, low = prob, -4.0

                def first_best(values, one, n):
                    link(V.tensor_reduce(gs[:, n, :], values, AX.X, ALU.max))
                    link(V.tensor_tensor(one, values, spread(n), ALU.is_equal))
                    link(V.tensor_tensor(one, one, rank_b, ALU.mult))
                    link(V.tensor_reduce(gs[:, n, :], one, AX.X, ALU.max))
                    link(V.tensor_tensor(one, rank_b, spread(n), ALU.is_equal))

                def value_at(one, n):
                    link(V.tensor_tensor(gate, prob, one, ALU.mult))
                    link(V.tensor_reduce(gs[:, n, :], gate, AX.X, ALU.add))

                first_best(pick, one1, 3)
                value_at(one1, 4)
                link(V.scalar_tensor_tensor(out=tmp, in0=one1, scalar=low, in1=pick, op0=ALU.mult, op1=ALU.add))
                first_best(tmp, one2, 3)
                value_at(one2, 5)
                link(V.tensor_tensor(gs[:, 0, :], gs[:, 4, :], gs[:, 5, :], ALU.add))
                if l == 0:
                    link(V.tensor_scalar(gs[:, 0, :], gs[:, 0, :], 1e-9, None, ALU.add))
                link(V.reciprocal(gs[:, 1, :], gs[:, 0, :]))
                link(V.tensor_tensor(tmp, one1, one2, ALU.add))
                link(V.tensor_tensor(tmp, tmp, prob, ALU.mult))
                V.tensor_tensor(gate, tmp, spread(1), ALU.mult).then_inc(sem(f"gates{l}"), 1)

            def gate_experts0():
                for u in range(E * 2 * 4):
                    e, half = u // 8, (u // 4) % 2
                    dve.wait_ge(sem("act_done0"), u + 1)
                    if u % 8 == 0:
                        dve.wait_ge(sem(f"gate_bc0_{e}"), 16)
                    if u >= 8:
                        dve.wait_ge(sem("down0"), u - 7)
                    V.tensor_tensor(hg_ring[:, u % 8, :], h_ring[:, u % 4, :], gate_bc[:, e, HALF * half:HALF * half + HALF],
                                    ALU.mult).then_inc(sem("gated0"), 1)

            def gate_experts1():
                for u in range(E * 2):
                    e, half = u // 2, u % 2
                    dve.wait_ge(sem("hidden1"), 4 * (u + 1))
                    for t in range(2):
                        n = 2 * u + t
                        slot = 2 * (u % 2) + t
                        dve.wait_ge(sem("act_done1"), n + 1)
                        if n >= 8:
                            dve.wait_ge(sem("down1"), n - 7)
                        V.scalar_tensor_tensor(out=hg_ring[:, n % 8, :], in0=ps[:, 2 + t, :],
                                               scalar=b1_col[:, 1, e * 4 + 2 + t:e * 4 + 3 + t], in1=h_ring[:, slot, :],
                                               op0=ALU.add, op1=ALU.mult).then_inc(sem("glu1"), 1)
                        dve.wait_ge(sem("glu1"), n + 1)
                        if half == 0 and t == 0:
                            dve.wait_ge(sem(f"gate_bc1_{e}"), 16)
                        V.tensor_tensor(hg_ring[:, n % 8, :], hg_ring[:, n % 8, :], gate_bc[:, e, HALF * half:HALF * half + HALF],
                                        ALU.mult).then_inc(sem("gated1"), 1)

            def ffn_out(l):
                dve.wait_ge(sem(f"turned_y{l}"), 2)
                y = flat(ps[:, 0:2, :])
                if l == 0:
                    link(V.tensor_tensor(flat(x_ln), y, flat(x_ln), ALU.add))
                    y = flat(x_ln)
                V.scalar_tensor_tensor(out=flat(x_sb), in0=y, scalar=g_tanh[:, 2 + l:3 + l], in1=flat(x_sb),
                                       op0=ALU.mult, op1=ALU.add).then_inc(sem(f"ffn_done{l}" if l == 0 else "x_final"), 1)

            def turn_mask():
                dve.wait_ge(sem("flag_ready"), 1)
                with dve.If(dve.value_load(flag[0:1, 0:1], min_val=0, max_val=1) > 0):
                    V.memset(big[:, NFULL * TQ // 4:], 0.0).then_inc(sem("mask_tail"), 1)
                    for c in range(NFULL // MCH + 1):
                        dve.wait_ge(sem("mask_again"), 16 * (c + 1))
                        rows, n = (P, MCH) if c < NFULL // MCH else (TAIL, 1)
                        dve.wait_ge(sem("mask_tail"), 1)
                        V.tensor_scalar(mask_n[0:rows, c * MCH:c * MCH + n, :],
                                        mask_stage[0][0:rows, 0:n * TQ].rearrange("p (t q) -> p t q", t=n), -1.0, 1.0,
                                        ALU.mult, ALU.add, saturate=False).then_inc(sem("mask_turned"), 1)
                with dve.Else():
                    dve.nop()

            V.memset(v_all[:, :, :, HD:VW], 1.0).then_inc(sem("v_init"), 1)
            V.memset(v_all[:, NFULL:NT, :, 0:HD], 0.0).then_inc(sem("v_init"), 1)
            V.memset(q_ring[2 * 32:MROW, :].bitcast(F32), 0.0).then_inc(sem("ring_set"), 1)
            dve.wait_ge(sem("x_in"), 16)
            layer_norm("q0", x_sb, x_n, "xn_q0")
            queries(0)
            split_keys()
            maxima(0)
            attention_out(0)
            dve.wait_ge(sem("small_in"), SMALL_IN)
            layer_norm("f0", x_sb, x_ln)
            set_flag()
            layer_norm("g0", x_ln, x_n)
            link(V.tensor_tensor(x_n[:, :, :], x_n[:, :, :], gb_row[:, 0:1, :].broadcast_to([P, QT, C]), ALU.mult))
            V.tensor_tensor(x_n[:, :, :], x_n[:, :, :], gb_row[:, 1:2, :].broadcast_to([P, QT, C]), ALU.add).then_inc(sem("xn_f0"), 1)
            top_two(0)
            gate_experts0()
            set_ring()
            ffn_out(0)
            dve.wait_ge(sem("ffn_done0"), 1)
            layer_norm("q1", x_sb, x_n, "xn_q1")
            queries(1)
            turn_mask()
            maxima(1)
            attention_out(1)
            layer_norm("f1", x_sb, x_n, "xn_f1")
            top_two(1)
            gate_experts1()
            ffn_out(1)

        @block.tensor
        def _(pe):
            def keys(l, c):
                w = chunk_w[c]
                if l == 0:
                    for c0, _ in CTX_CHUNKS:
                        if c * HALF == c0:
                            pe.wait_ge(sem(f"ctx_in{c0}"), 16)
                if c >= 2:
                    pe.wait_ge(sem(f"k_evac{l}"), 2 * (c - 1))
                pe.matmul(ps[:, c % 2, 0:w], w_att[:, l, 1, :], ctx_t[:, HALF * c:HALF * c + w],
                          start=True, stop=True).then_inc(sem(f"k_proj{l}"), 1)

            def values(l, c, bank, banks):
                if c >= banks:
                    pe.wait_ge(sem(f"v_set{l}"), c - banks + 1)
                for t in range(4 * c, min(4 * c + 4, NT)):
                    mm = pe.matmul(ps[0:width(t), bank + c % banks, P * (t % 4):P * (t % 4) + P],
                                   ctx_t[:, P * t:P * t + width(t)], w_att[:, l, 2, :], start=True, stop=True)
                mm.then_inc(sem(f"v_proj{l}"), 1)

            def turn(tag, src, bank, after, n):
                for t in range(QT):
                    if t == 0 or n == QT:
                        pe.wait_ge(sem(after), n if n != QT else t + 1)
                    mm = pe.transpose(ps[:, bank + t // 4, P * (t % 4):P * (t % 4) + P], src(t), ident_f[:, :])
                    if t % 4 == 3:
                        mm.then_inc(sem(f"turned_{tag}"), 1)

            def queries(l):
                turn(f"q{l}", lambda t: x_n[:, t, :], 4, f"xn_q{l}", QT)
                for half in range(2):
                    pe.wait_ge(sem(f"copied_q{l}"), half + 1)
                    pe.matmul(ps[:, 6 + half, :], w_att[:, l, 0, :], x_t[:, HALF * half:HALF * half + HALF],
                              start=True, stop=True).then_inc(sem(f"q_proj{l}"), 1)

            def key(koff, t, rows):
                return k_ring[0:rows, bass.ds(koff + P * t, width(t))]

            def query(qoff, half, rows):
                return q_ring[0:rows, bass.ds(qoff + HALF * half, HALF)]

            def score(dst, koff, qoff, t, half, rows, masked):
                k = width(t)
                if masked:
                    pe.matmul(dst[0:k], neg_i[:, 0:k], mask_n[:, t, HALF * half:HALF * half + HALF], start=True, stop=False)
                return pe.matmul(dst[0:k], key(koff, t, rows), query(qoff, half, rows), start=not masked, stop=True)

            def max_tile(l, unit, slot, koff, qoff, t, masked):
                if not (isinstance(unit, int) and unit < 2):
                    wait_apart(pe, "pe", sem(f"mx_done{l}"), unit - 1, masked or t == NT - 1)
                for half in range(2):
                    mm = score(mx(slot)[:, half, :], koff, qoff, t, half, ROWS_MAX, masked)
                mm.then_inc(sem(f"mx_filled{l}"), 1)

            def turn_max(l, h, unit, slot):
                pe.wait_ge(sem(f"mx_done{l}"), unit - 1)
                pe.wait_ge(sem(f"m_joined{l}"), h + 1)
                for t in range(QT):
                    mm = pe.transpose(mx(slot)[:, t // 4, P * (t % 4):P * (t % 4) + P], m_join[:, P * t:P * t + P], ident_f[:, :])
                mm.then_inc(sem(f"mx_filled{l}"), 1)

            def turn_rows(l, h, unit, slot):
                pe.wait_ge(sem(f"mx_done{l}"), unit - 1)
                pe.wait_ge(sem(f"m_split{l}"), h * 4 + 4)
                rows = ps[:, 2 * slot, :].bitcast(BF16)
                for t in range(QT):
                    mm = pe.transpose(rows[:, P * t:P * t + P], m_pad[:, t, :], ident_b[:, :])
                mm.then_inc(sem(f"mx_filled{l}"), 1)

            def turn_out(l, h, unit, slot):
                pe.wait_ge(sem(f"mx_done{l}"), unit - 1)
                pe.wait_ge(sem(f"o_raw{l}"), h + 1)
                for c in range(2):
                    mm = pe.transpose(mx(slot)[:, 0, P * c:P * c + P], o_raw[:, P * c:P * c + P], ident_f[:, :])
                mm.then_inc(sem(f"mx_filled{l}"), 1)

            def exp_unit(l, h, koff, qoff, u, masked):
                t, half = u // 2, u % 2
                banks = exp_banks(l, h)
                late = len(banks) - EXB
                if u < EXB or u >= len(banks):
                    wait_apart(pe, "pe", sem(f"exp_done{l}"), h * (2 * NT) + (u + 1 - (late if u >= EXB else 0)),
                               masked or t == NT - 1)
                score(ps[:, banks[u % len(banks)], :], koff, qoff, t, half, ROWS_EXP, masked).then_inc(sem(f"scored{l}"), 1)

            def weigh(l, h, t):
                k = width(t)
                if t == 0:
                    pe.wait_ge(sem(f"o_raw{l}"), h + 1)
                for n, (t0, _) in enumerate(V_CHUNKS):
                    if t == t0:
                        pe.wait_ge(sem(f"v_head{l}"), h * len(V_CHUNKS) + (n + 1))
                wait_apart(pe, "pe", sem(f"exp_done{l}"), h * (2 * NT) + (2 * t + 2 + EXB), t == NT - 1)
                for g in range(QG):
                    mm = pe.matmul(ps[32 * g:32 * g + VW, 7, 0:QGW], v_head[0:k, t, :], probs[0:k, p_slot(t), QGW * g:QGW * g + QGW],
                                   start=(t == 0), stop=(t == NT - 1))
                mm.then_inc(sem(f"pv_done{l}"), 1)

            def place(n, w):
                return n % RING * w if isinstance(n, int) else pe.snap((n % RING) * w)

            def one_unit(l, h, kind, unit, slot, at, masked):
                if kind == "out":
                    turn_out(l, h, unit, slot)
                elif kind == "turn":
                    turn_max(l, h + 1, unit, slot)
                elif kind == "rows":
                    turn_rows(l, h + 1, unit, slot)
                else:
                    what, t = kind
                    koff, qoff = at[0 if what == "max" else 1]
                    max_tile(l, unit, slot, koff, qoff, t, masked)

            def head(l, h, base, masked, steps, keys_values=False):
                at = [(place(h + n, TK), place(h + n, TQ)) for n in range(3)]
                wait_apart(pe, "pe", sem(f"mx_done{l}"), base - AFTER_ROWS if not isinstance(h, int) or h < H - 1 else base, masked)
                j = 0
                for s in range(NSTEP):
                    scores = list(range(2 * STEP * s, min(2 * STEP * (s + 1), 2 * NT)))
                    if ("next", 0) in steps[s]:
                        pe.wait_ge(sem(f"head_in{l}"), h * HEAD_IN + 3 * HEAD_IN)
                    among, within, after = steps[s][:1], steps[s][1:-1], steps[s][1:][-1:]
                    for u in scores[:EXB]:
                        exp_unit(l, h, *at[0], u, masked)
                    for kind in among:
                        one_unit(l, h, kind, base + j, j % 2, at[1:], masked)
                        j += 1
                    if keys_values and (s == 1 or s and s % 2 == 0):
                        c = s // 2
                        if c == 0:
                            pe.wait_ge(sem("att_w_in1"), ATT_IN)
                            pe.wait_ge(sem("mx_done0"), LAST + 1)
                        keys(1, c)
                        values(1, c, 2, 2)
                    for u in scores[EXB:]:
                        exp_unit(l, h, *at[0], u, masked)
                    for t in range(STEP * (s - 1), STEP * s) if s else ():
                        weigh(l, h, t)
                        for kind in within if t % STEP == 0 else after:
                            one_unit(l, h, kind, base + j, j % 2, at[1:], masked)
                            j += 1
                for t in range(STEP * (NSTEP - 1), NT):
                    weigh(l, h, t)

            def attention(l, masked):
                pe.wait_ge(sem(f"head_in{l}"), FIRST_IN[l][0])
                for unit, kind in enumerate([("max", t) for t in range(NT)] + ENDING_UNITS):
                    if kind == ("next", 0):
                        pe.wait_ge(sem(f"head_in{l}"), FIRST_IN[l][1])
                    one_unit(l, -1, kind, unit, (unit + FIRST) % 2, [(0, 0), (TK, TQ)], masked)
                    if l == 0 and unit % 4 == 3 and unit // 4 < NCH:
                        values(0, unit // 4, 4, 4)
                if l == 0:
                    pe.wait_ge(sem("v_set0"), NCH + 1)
                pe.matmul(ps[:, 7, 0:QGW], ones_b[:, 0:P], ones_b[:, 0:QGW], start=True, stop=True).then_inc(sem(f"pv_done{l}"), NT)
                with pe.Fori(0, LOOP) as h:
                    head(l, h, pe.snap(h * MXU + FIRST), masked, mx_steps(True))
                head(l, H - 2, LAST2, masked, mx_steps(False))
                head(l, H - 1, LAST, masked, [["out"] if s == 1 else [] for s in range(NSTEP)], l == 0)
                if l == 0:
                    pe.wait_ge(sem("v_set1"), NCH + 1)
                turn_out(l, H, LAST + 1, 1)

            def attention_out(l):
                turn(f"o{l}", lambda t: o_all[:, t, HD:HD + C], 0, f"o_biased{l}", 2)
                for t in range(QT):
                    if t % 4 == 0:
                        pe.wait_ge(sem(f"copied_o{l}"), t // 4 + 1)
                    mm = pe.matmul(ps[:, 2 + t // 4, P * (t % 4):P * (t % 4) + P], x_t[:, P * t:P * t + P], w_att[:, l, 3, :],
                                   start=True, stop=True)
                    if t % 4 == 3:
                        mm.then_inc(sem(f"o_proj{l}"), 1)

            def gating(l):
                turn(f"f{l}", lambda t: x_n[:, t, :], 0, f"xn_f{l}", (1, QT)[l])
                pe.wait_ge(sem("small_in"), SMALL_IN)
                for t in range(QT):
                    if t % 4 == 0:
                        pe.wait_ge(sem(f"copied_f{l}"), t // 4 + 1)
                    mm = pe.matmul(ps[:, 7, E * t:E * t + E], x_t[:, P * t:P * t + P], w_gate[:, l, :], start=True, stop=True)
                mm.then_inc(sem(f"logits{l}"), 1)

            def turn_gates(l):
                pe.wait_ge(sem(f"gates{l}"), 1)
                for t in range(QT):
                    mm = pe.transpose(ps[0:E, 6 + t // 4, P * (t % 4):P * (t % 4) + P], ga[:, 4, t, :], ident_f[:, :])
                mm.then_inc(sem(f"gate_turned{l}"), 1)

            def experts(l):
                w1, w2, nd = (w1_0, w2_0, 4) if l == 0 else (w1_1, w2_1, 2)
                pe.wait_ge(sem(f"experts_in{l}"), 32)

                def up(u):
                    e, half = u // 2, u % 2
                    for t in range(4):
                        n = 4 * u + t
                        if u >= 1 and l == 0:
                            pe.wait_ge(sem("act_done0"), n - 3)
                        if u >= 1 and l == 1 and t < 2:
                            pe.wait_ge(sem("act_done1"), 2 * (u - 1) + t + 1)
                        if u >= 1 and l == 1 and t >= 2:
                            pe.wait_ge(sem("glu1"), 2 * (u - 1) + t - 1)
                        pe.matmul(ps[:, t, :], w1[:, e, P * t:P * t + P], x_t[:, HALF * half:HALF * half + HALF],
                                  start=True, stop=True).then_inc(sem(f"hidden{l}"), 1)

                def down(u):
                    e, half = u // 2, u % 2
                    for t in range(nd):
                        n = nd * u + t
                        pe.wait_ge(sem(f"gated{l}"), n + 1)
                        mm = pe.matmul(ps[:, 4 + half, :], w2[:, e, t, :], hg_ring[:, n % 8, :],
                                       start=(e == 0 and t == 0), stop=False)
                        mm.then_inc(sem(f"down{l}"), 1)

                for u in range(2 * E):
                    up(u)
                    if u == 0:
                        turn_gates(l)
                    if u:
                        down(u - 1)
                down(2 * E - 1)
                pe.wait_ge(sem(f"gate_t{l}"), 1)
                for half in range(2):
                    mm = pe.matmul(ps[:, 4 + half, :], b2_sb[:, l, :], gate_t[:, HALF * half:HALF * half + HALF],
                                   start=False, stop=True)
                    mm.then_inc(sem(f"y_sum{l}"), 1)

            def y_out(l):
                for t in range(QT):
                    if t % 4 == 0:
                        pe.wait_ge(sem(f"y_t{l}"), t // 4 + 1)
                    mm = pe.transpose(ps[:, t // 4, P * (t % 4):P * (t % 4) + P], y_t[:, P * t:P * t + P], ident_f[:, :])
                    if t % 4 == 3:
                        mm.then_inc(sem(f"turned_y{l}"), 1)

            pe.wait_ge(sem("ident"), 2)
            pe.wait_ge(sem("ones_set"), 1)
            pe.wait_ge(sem("att_w_in0"), ATT_IN)
            queries(0)
            for c in range(NCH):
                keys(0, c)
            attention(0, False)
            pe.wait_ge(sem("mask_tot"), 1)
            pe.wait_ge(sem("rank"), E + 3)
            pe.matmul(ps[0:1, 7, 0:1], m_tot[:, :], ones_f[:, :], start=True, stop=True).then_inc(sem("mask_all"), 1)
            attention_out(0)
            gating(0)
            experts(0)
            y_out(0)
            queries(1)
            pe.wait_ge(sem("flag_ready"), 1)
            with pe.If(pe.value_load(flag[0:1, 0:1], min_val=0, max_val=1) > 0):
                pe.wait_ge(sem("mask_turned"), NFULL // MCH + 1)
                attention(1, True)
            with pe.Else():
                attention(1, False)
            attention_out(1)
            gating(1)
            experts(1)
            y_out(1)


def kernel(x, ctx_1024, mask_Bx1xSxS2_bf1, g_xattn, g_ffn, **w):
    import concourse.bacc as bacc
    from concourse.bass_utils import run_bass_kernel_spmd

    nc = bacc.Bacc("TRN2", target_bir_lowering=False, num_devices=1)
    lay = np.ascontiguousarray
    arrays = {
        "x": lay(np.asarray(x).reshape(TQ, C)),
        "ctx_t": lay(np.asarray(ctx_1024).reshape(TK, C).T),
        "mask_t": lay(np.asarray(mask_Bx1xSxS2_bf1).reshape(TQ, TK).view(np.uint8).T),
        "g_xattn": lay(g_xattn), "g_ffn": lay(g_ffn),
        "gamma": lay(w["L0_ffn_gamma"]), "beta": lay(w["L0_ffn_beta"]), "br": lay(w["L1_ffn_br"]),
        "w_gate0": lay(np.asarray(w["L0_ffn_Wg"]).T), "w_gate1": lay(w["L1_ffn_Wr"]),
    }
    for l in range(2):
        for n in "qkvo":
            arrays[f"w{n}{l}"] = lay(np.asarray(w[f"L{l}_xattn_W{n}"]).T)
            bias = np.asarray(w[f"L{l}_xattn_b{n}"])
            arrays[f"b{n}{l}"] = lay(bias.reshape(C, 1) if n in "qk" else bias)
        arrays[f"w1_{l}"] = lay(w[f"L{l}_ffn_W1"])
        arrays[f"w2_{l}"] = lay(w[f"L{l}_ffn_W2"])
        arrays[f"b1_{l}"] = lay(np.asarray(w[f"L{l}_ffn_b1"]).reshape(E * FF // P, P).T)
        arrays[f"b2_{l}"] = lay(w[f"L{l}_ffn_b2"])
    arrays = {f"in_{n}": v for n, v in arrays.items()}
    args = {n[3:]: nc.dram_tensor(n, v.shape, mybir.dt.from_np(v.dtype), kind="ExternalInput").ap() for n, v in arrays.items()}
    out = nc.dram_tensor("out", [TQ, C], F32, kind="ExternalOutput").ap()
    block_kernel(nc, args, out)
    r = run_bass_kernel_spmd(nc, [arrays], core_ids=[0])
    return r.results[0]["out"].reshape(1, TQ, C)
```
